# Optimizing a Trainium2 kernel written in Bass

```python
import numpy as np
import jax
import jax.numpy as jnp

def _softmax(x, axis=-1):
    return jax.nn.softmax(x, axis=axis)

def _gelu(x):
    return jax.nn.gelu(x, approximate=True)

def _silu(x):
    return jax.nn.silu(x)

def _sigmoid(x):
    return jax.nn.sigmoid(x)

def _layernorm(x, axis=-1, eps=1e-05):
    m = jnp.mean(x, axis=axis, keepdims=True)
    v = jnp.var(x, axis=axis, keepdims=True)
    return (x - m) / jnp.sqrt(v + eps)

def _scatter_add(tgt, idx, src, axis=0):
    return tgt.at[idx].add(src)

def _segment_sum(src, seg, n):
    return jax.ops.segment_sum(src, seg, n)
kernel_name = 'mk_macaron_d1_jaxref_r8_598669'

def setup_inputs(seed: int=0):
    np.random.seed(seed)
    _w = jnp.asarray

    def _L0_attn_setup():
        import jax, jax.numpy as jnp
        import numpy as np
        B_SZ, L, H, P = (4, 512, 128, 128)
        R_MIN, R_MAX, MAX_PHASE = (0.0, 1.0, 6.28)
        key = jax.random.key(seed)
        ks = jax.random.split(key, 8)
        inputs = jax.random.normal(ks[0], (B_SZ, L, H), dtype=jnp.float32)
        u1 = jax.random.uniform(ks[1], (P,))
        nu = -0.5 * jnp.log(u1 * (R_MAX ** 2 - R_MIN ** 2) + R_MIN ** 2)
        nu_log = jnp.log(nu)
        u2 = jax.random.uniform(ks[2], (P,))
        theta_log = jnp.log(MAX_PHASE * u2)
        B_re = jax.random.normal(ks[3], (P, H)) * jnp.sqrt(0.5 / P)
        B_im = jax.random.normal(ks[4], (P, H)) * jnp.sqrt(0.5 / P)
        C_re = jax.random.normal(ks[5], (H, P)) * jnp.sqrt(1.0 / H)
        C_im = jax.random.normal(ks[6], (H, P)) * jnp.sqrt(1.0 / H)
        D = jax.random.normal(ks[7], (H,))
        diag_lambda = jnp.exp(-jnp.exp(nu_log) + 1j * jnp.exp(theta_log))
        gamma_log = jnp.log(jnp.sqrt(1.0 - jnp.abs(diag_lambda) ** 2))
        return {'inputs': inputs, 'nu_log': nu_log.astype(jnp.float32), 'theta_log': theta_log.astype(jnp.float32), 'B_re': B_re.astype(jnp.float32), 'B_im': B_im.astype(jnp.float32), 'C_re': C_re.astype(jnp.float32), 'C_im': C_im.astype(jnp.float32), 'D': D.astype(jnp.float32), 'gamma_log': gamma_log.astype(jnp.float32)}
    _L0_attn_in = _L0_attn_setup()

    def _L0_ffn_setup():
        import jax, jax.numpy as jnp
        import numpy as np
        DIM = 128
        HIDDEN = 512
        N_EXPERTS = 8
        K = 2
        TEMP = 1.0

        def _expert_ffn(xf, wa, ba, wb, bb):
            h = xf @ wa.T + ba
            h1, h2 = jnp.split(h, 2, axis=-1)
            h = jax.nn.silu(h1) * h2
            return h @ wb.T + bb
        key = jax.random.key(seed)
        ks = jax.random.split(key, 7)
        s = 0.02
        x = jax.random.normal(ks[0], (4, 256, DIM), dtype=jnp.float32)
        router_w = jax.random.normal(ks[1], (N_EXPERTS, DIM), dtype=jnp.float32) * s
        router_b = jnp.zeros((N_EXPERTS,), dtype=jnp.float32)
        w1 = jax.random.normal(ks[2], (N_EXPERTS, 2 * HIDDEN, DIM), dtype=jnp.float32) * s
        b1 = jnp.zeros((N_EXPERTS, 2 * HIDDEN), dtype=jnp.float32)
        w2 = jax.random.normal(ks[3], (N_EXPERTS, DIM, HIDDEN), dtype=jnp.float32) * s
        b2 = jnp.zeros((N_EXPERTS, DIM), dtype=jnp.float32)
        return {'x': x, 'router_w': router_w, 'router_b': router_b, 'w1': w1, 'b1': b1, 'w2': w2, 'b2': b2}
    _L0_ffn_in = _L0_ffn_setup()
    _d = {'L0_attn_inputs': _L0_attn_in['inputs'], 'L0_attn_nu_log': _L0_attn_in['nu_log'], 'L0_attn_theta_log': _L0_attn_in['theta_log'], 'L0_attn_B_re': _L0_attn_in['B_re'], 'L0_attn_B_im': _L0_attn_in['B_im'], 'L0_attn_C_re': _L0_attn_in['C_re'], 'L0_attn_C_im': _L0_attn_in['C_im'], 'L0_attn_D': _L0_attn_in['D'], 'L0_attn_gamma_log': _L0_attn_in['gamma_log'], 'L0_ffn_router_w': _L0_ffn_in['router_w'], 'L0_ffn_router_b': _L0_ffn_in['router_b'], 'L0_ffn_w1': _L0_ffn_in['w1'], 'L0_ffn_b1': _L0_ffn_in['b1'], 'L0_ffn_w2': _L0_ffn_in['w2'], 'L0_ffn_b2': _L0_ffn_in['b2']}
    _x0 = _d['L0_attn_inputs']
    _d['L0_attn_inputs'] = jax.random.normal(jax.random.fold_in(jax.random.key(seed), 1), (4, 1024, 128), dtype=_x0.dtype)
    del _x0
    return _d

def reference(L0_attn_inputs, L0_attn_nu_log, L0_attn_theta_log, L0_attn_B_re, L0_attn_B_im, L0_attn_C_re, L0_attn_C_im, L0_attn_D, L0_attn_gamma_log, L0_ffn_router_w, L0_ffn_router_b, L0_ffn_w1, L0_ffn_b1, L0_ffn_w2, L0_ffn_b2):

    def _L0_attn_ref(inputs, nu_log, theta_log, B_re, B_im, C_re, C_im, D, gamma_log):
        import jax, jax.numpy as jnp
        import numpy as np
        B_SZ, L, H, P = (4, 512, 128, 128)
        R_MIN, R_MAX, MAX_PHASE = (0.0, 1.0, 6.28)
        batch_size, input_length, _ = inputs.shape
        Lambda = jnp.exp(-jnp.exp(nu_log) + 1j * jnp.exp(theta_log))
        Bmat = B_re + 1j * B_im
        Cmat = C_re + 1j * C_im
        gamma = jnp.exp(gamma_log)
        B_norm = Bmat * gamma[:, None]

        def apply_step(elem_i, elem_j):
            a_i, bu_i = elem_i
            a_j, bu_j = elem_j
            return (a_j * a_i, a_j * bu_i + bu_j)
        Ls = jnp.broadcast_to(Lambda, (batch_size, input_length, Lambda.shape[0]))
        Bu = jnp.einsum('ph,blh->blp', B_norm, inputs.astype(B_norm.dtype))
        _, xs = jax.lax.associative_scan(apply_step, (Ls, Bu), axis=1)
        Cx = jnp.einsum('hp,blp->blh', Cmat, xs).real
        Du = D * inputs
        return Cx + Du

    def _L0_ffn_ref(x, router_w, router_b, w1, b1, w2, b2):
        import jax, jax.numpy as jnp
        import numpy as np
        DIM = 128
        HIDDEN = 512
        N_EXPERTS = 8
        K = 2
        TEMP = 1.0

        def _expert_ffn(xf, wa, ba, wb, bb):
            h = xf @ wa.T + ba
            h1, h2 = jnp.split(h, 2, axis=-1)
            h = jax.nn.silu(h1) * h2
            return h @ wb.T + bb
        b, t, d = x.shape
        logits = (x @ router_w.T + router_b) / TEMP
        topk_val, topk_idx = jax.lax.top_k(logits, K)
        weights = jax.nn.softmax(topk_val, axis=-1)
        xf = x.reshape(-1, d)
        outs = jax.vmap(_expert_ffn, in_axes=(None, 0, 0, 0, 0))(xf, w1, b1, w2, b2)
        outs = jnp.transpose(outs, (1, 0, 2))
        idx = topk_idx.reshape(-1, K)
        gathered = jnp.take_along_axis(outs, idx[:, :, None], axis=1)
        combined = (gathered * weights.reshape(-1, K, 1)).sum(axis=1)
        return combined.reshape(b, t, d)
    x = L0_attn_inputs
    x = x + 0.5 * _L0_ffn_ref(_layernorm(x, axis=-1), L0_ffn_router_w, L0_ffn_router_b, L0_ffn_w1, L0_ffn_b1, L0_ffn_w2, L0_ffn_b2)
    x = x + _L0_attn_ref(_layernorm(x, axis=-1), L0_attn_nu_log, L0_attn_theta_log, L0_attn_B_re, L0_attn_B_im, L0_attn_C_re, L0_attn_C_im, L0_attn_D, L0_attn_gamma_log)
    x = x + 0.5 * _L0_ffn_ref(_layernorm(x, axis=-1), L0_ffn_router_w, L0_ffn_router_b, L0_ffn_w1, L0_ffn_b1, L0_ffn_w2, L0_ffn_b2)
    return x

_drawn_inputs = setup_inputs


def setup_inputs(seed=0):
    import zlib

    import numpy as np

    out = dict(_drawn_inputs(seed))
    spreads = {'L0_ffn_router_b': (0.0, 0.355), 'L0_ffn_b1': (0.0, 0.8), 'L0_ffn_b2': (0.0, 0.1)}
    factors = {'L0_ffn_w1': 8.0, 'L0_ffn_w2': 8.0}
    for name, (base, spread) in spreads.items():
        noise = np.random.default_rng([zlib.crc32(name.encode()), seed]).standard_normal(out[name].shape)
        drawn = base * np.exp(spread * noise) if base else spread * noise
        out[name] = jnp.asarray(drawn.astype(out[name].dtype))
    for name, factor in factors.items():
        out[name] = (out[name] * factor).astype(out[name].dtype)
    return out
```

```python
from contextlib import ExitStack

import concourse.bass as bass
from concourse import mybir

FP32 = mybir.dt.float32
FP16 = mybir.dt.float16
I32 = mybir.dt.int32
ACT = mybir.ActivationFunctionType
ALU = mybir.AluOpType
AX = mybir.AxisListType.X

P = 128
BATCH, SEQ = 4, 1024
TOK = BATCH * SEQ
GT = SEQ // P
NE, HID, TOPK = 8, 512, 2
HB = HID // P
SLOT = 256
NTILE = TOPK * TOK // SLOT + NE - 1
REG = TOK + SLOT
ROWW = P + 2
WS = 16.0
OUTSIDE = 1 << 20
BIG = 3.0e38
TWO_PI = 6.283185307179586
PI = 3.14159274
EPS = 1e-5
BUFS = 2
H0, H1 = 1, (NTILE - 1) // 2
HALF = SEQ // 2


def macaron_block(nc, x, nu_log, theta_log, b_re, b_im, c_re_t, c_im_t, d_vec, gamma_log,
                  router_t, router_b, w1_t, b1_t, w2_t, b2, out):
    ctx = ExitStack()
    with ctx:
        def sb(name, shape, dt=FP32):
            return ctx.enter_context(nc.sbuf_tensor(name, shape, dt))

        def sem(name):
            return ctx.enter_context(nc.semaphore(name))

        rows_dram = [nc.dram_tensor(f"rows{f}", [NE * REG + SLOT, ROWW], FP32, kind="Internal").ap() for f in range(2)]
        y_dram = [nc.dram_tensor(f"y{f}", [TOPK * TOK, P], FP32, kind="Internal").ap() for f in range(2)]

        xres = sb("xres", [P, BATCH, GT, P])
        yin = sb("yin", [P, 2, TOPK, GT, P])
        xn = sb("xn", [P, 2, GT, P])
        xnt = sb("xnt", [P, 2, SEQ])
        rows = sb("rows", [P, TOPK, BATCH, GT, ROWW])
        bn = sb("bn", [P, GT, 6])
        mv = sb("mv", [P, 2, GT, 2])
        std = sb("std", [P, 2, GT])
        rstd = sb("rstd", [P, 2, GT])
        ident = sb("ident", [P, P])
        ident16 = sb("ident16", [P, P], FP16)
        before = sb("before", [P, P], FP16)
        ones16 = sb("ones16", [P, P], FP16)
        w1h = sb("w1h", [P, NE * 2 * HID], FP16)
        w1l = sb("w1l", [P, NE * 2 * HID], FP16)
        w2h = sb("w2h", [P, NE * HB * P], FP16)
        w2l = sb("w2l", [P, NE * HB * P], FP16)
        wst = sb("wst", [P, 2, 2 * HID + HB * P])
        b1g = sb("b1g", [P, NE, 2 * HB])
        b1u = sb("b1u", [P, NE * HB])
        b2b = sb("b2b", [P, NE * P])
        rwt = sb("rwt", [P, NE])
        rbb = sb("rbb", [P, NE])
        eps_c = sb("eps_c", [P, 1])
        rev_i = sb("rev_i", [P, 2 * NE + NTILE], I32)
        rev_f = sb("rev_f", [P, 2 * NE + NTILE])
        dest_i = sb("dest_i", [P, TOPK, BATCH, GT], I32)
        lg = sb("lg", [P, GT, NE])
        m1 = sb("m1", [P, GT])
        m2 = sb("m2", [P, GT])
        rr = sb("rr", [P, GT])
        oh1 = sb("oh1", [P, GT, NE])
        oh2 = sb("oh2", [P, GT, NE])
        tmp8 = sb("tmp8", [P, GT, NE])
        oh = sb("oh", [P, 2, GT, NE], FP16)
        seen = sb("seen", [P, 2, BATCH + 1, NE], FP16)
        seen1 = sb("seen1", [P, NE])
        dif = sb("dif", [P, 2, GT])
        edif = sb("edif", [P, 2, GT])
        den = sb("den", [P, GT])
        wk = sb("wk", [P, TOPK, GT])
        slotf = sb("slotf", [P, GT, NE])
        slot1 = sb("slot1", [P, GT])
        slot_i = sb("slot_i", [P, TOPK, 2, BATCH, GT], I32)
        cnt = sb("cnt", [P, NE])
        cnt_i = sb("cnt_i", [P, NE], I32)
        ntile = sb("ntile", [P, NE])
        upto = sb("upto", [P, NE])
        ones8 = sb("ones8", [P, NE])
        base8 = sb("base8", [P, NE])
        toff = sb("toff", [P, NTILE])
        tex = sb("tex", [P, NTILE])
        toff_i = sb("toff_i", [P, 2, NTILE], I32)
        tex_i = sb("tex_i", [P, 2, NTILE], I32)
        pad_i = sb("pad_i", [P, 2, NE], I32)
        padrow = sb("padrow", [P, 2, ROWW])
        xt = sb("xt", [P, BUFS, 2, ROWW])
        meta = sb("meta", [P, NTILE, 2, 2])
        dest = sb("dest", [P, BUFS, 2], I32)
        weight = sb("weight", [P, BUFS, 2])
        xt_t = sb("xt_t", [P, BUFS, 2, SLOT], FP16)
        gate = sb("gate", [P, HB, SLOT])
        act = sb("act", [P, HB, SLOT])
        acth = sb("acth", [P, BUFS, HB, SLOT], FP16)
        actl = sb("actl", [P, BUFS, HB, SLOT], FP16)
        ysum = sb("ysum", [P, BUFS, 2, P])
        yout = sb("yout", [P, BUFS, 2, P])
        bst = sb("bst", [P, 2, P])
        bt = sb("bt", [P, 2, P])
        ct_re = sb("ct_re", [P, P])
        ct_im = sb("ct_im", [P, P])
        nct_im = sb("nct_im", [P, P])
        nct_re = sb("nct_re", [P, P])
        diag_d = sb("diag_d", [P, P])
        vec = sb("vec", [P, 4])
        lam = sb("lam", [P, 16])
        lam_i = sb("lam_i", [P, 1], I32)
        ctab = sb("ctab", [P, SEQ])
        stab = sb("stab", [P, SEQ])
        ge_hi, ge_lo = [b[:, :, :].rearrange("p j s -> p (j s)")[:, 0:NTILE * NE].rearrange("p (t e) -> p t e", e=NE)
                        for b in (gate, act)]
        rot = [half[:, 2 * i:2 * i + 2, :].rearrange("p j s -> p (j s)") for half in (gate, act) for i in range(2)]
        yre, yim = wst[:, 0, 0:SEQ], wst[:, 1, 0:SEQ]
        prod = sb("prod", [P, 4, SEQ])

        bank = [ctx.enter_context(nc.psum_tensor(f"bank{i}", [P, 512], FP32)) for i in range(8)]
        up_ps, y_ps, t_ps = bank[0:4], bank[4:6], bank[6:8]
        rows16 = rows[:, :, :, :, 0:P].bitcast(FP16)
        xt16 = xt[:, :, :, 0:P].bitcast(FP16)
        logit_ps, rank_ps = bank[2], bank[3]
        t16 = [t[:, :].bitcast(FP16) for t in t_ps]

        s_xin = [sem(f"s_xin{g}") for g in range(BATCH)]
        s_small = sem("s_small")
        s_w = [sem(f"s_w{i}") for i in range(2)]
        s_pool = sem("s_pool")
        s_const = sem("s_const")
        s_wh = sem("s_wh")
        s_wl = sem("s_wl")
        s_b1u = sem("s_b1u")
        s_var = sem("s_var")
        s_std = sem("s_std")
        s_xn = sem("s_xn")
        s_tr = sem("s_tr")
        s_xnt = sem("s_xnt")
        s_hi = sem("s_hi")
        s_row = sem("s_row")
        s_logit = sem("s_logit")
        s_lg = sem("s_lg")
        s_dif = sem("s_dif")
        s_edif = sem("s_edif")
        s_oh = sem("s_oh")
        s_rank = sem("s_rank")
        s_slot = sem("s_slot")
        s_sent = sem("s_sent")
        s_cnt = sem("s_cnt")
        s_tab = sem("s_tab")
        s_pad = sem("s_pad")
        s_chain = sem("s_chain")
        s_xt = [sem(f"s_xt{i}") for i in range(BUFS)]
        s_t = sem("s_t")
        s_xtt = sem("s_xtt")
        s_meta = sem("s_meta")
        s_up = sem("s_up")
        s_gate = sem("s_gate")
        s_act = sem("s_act")
        s_acth = sem("s_acth")
        s_actl = sem("s_actl")
        s_down = sem("s_down")
        s_ysum = sem("s_ysum")
        s_metab = sem("s_metab")
        s_yout = sem("s_yout")
        s_ygo = sem("s_ygo")
        s_ysent = [sem(f"s_ysent{i}") for i in range(BUFS)]
        s_yin = [sem(f"s_yin{i}") for i in range(2)]
        s_x1 = sem("s_x1")
        s_lam = sem("s_lam")
        s_lama = sem("s_lama")
        s_bsc = sem("s_bsc")
        s_btr = sem("s_btr")
        s_bt = sem("s_bt")
        s_bu = sem("s_bu")
        s_bud = sem("s_bud")
        s_prod = sem("s_prod")
        s_cx = sem("s_cx")
        s_x2 = sem("s_x2")
        s_x3 = sem("s_x3")
        s_out = sem("s_out")

        order = [("ffn", 0, g) for g in range(BATCH)]
        order += [("lru", 0, 0), ("lru", 0, 1), ("ffn", 1, 0), ("lru", 0, 2), ("ffn", 1, 1), ("lru", 0, 3),
                  ("ffn", 1, 2), ("ffn", 1, 3)]
        first_middle = BATCH

        def even_odd(f, par, pairs):
            return f * ((NTILE + 1) // 2 if par == 0 else NTILE // 2) + pairs

        block = ctx.enter_context(nc.Block())

        @block.sync
        def _(sp):
            small = [(rwt[:, :], router_t), (rbb[:, :], router_b.partition_broadcast(P)),
                     (b1g[:, :, :], b1_t), (b2b[:, :], b2.partition_broadcast(P)),
                     (bst[:, 0, :], b_re), (bst[:, 1, :], b_im), (ct_re[:, :], c_re_t), (ct_im[:, :], c_im_t),
                     (vec[:, 0:1], nu_log), (vec[:, 1:2], theta_log), (vec[:, 2:3], d_vec), (vec[:, 3:4], gamma_log)]
            for g in range(BATCH):
                sp.dma_start(xres[:, g, :, :], x[g].rearrange("(t p) d -> p t d", p=P)).then_inc(s_xin[g], 16)
                if g == 0:
                    for dst, src in small:
                        sp.dma_start(dst, src).then_inc(s_small, 16)
            for e in range(NE):
                if e >= 2:
                    sp.wait_ge(s_wl, 2 * (e - 1))
                sp.dma_start(wst[:, e % 2, 0:2 * HID], w1_t[:, e, :]).then_inc(s_w[e % 2], 16)
                sp.dma_start(wst[:, e % 2, 2 * HID:], w2_t[:, e, :]).then_inc(s_w[e % 2], 16)

            for f in range(2):
                sp.wait_ge(s_tab, f + 1)
                sp.wait_ge(s_sent, 16 * TOPK * BATCH * GT * (f + 1))
                for e in range(NE):
                    row0 = sp.value_load(pad_i[0:1, f, e:e + 1], min_val=0, max_val=NE * REG - SLOT)
                    sp.dma_start(rows_dram[f][bass.ds(row0, SLOT), :].rearrange("(p r) w -> p r w", r=2),
                                 padrow[:, :, :]).then_inc(s_pad, 16)
                sp.dma_start(rows_dram[f][NE * REG:NE * REG + SLOT, :].rearrange("(p r) w -> p r w", r=2),
                             padrow[:, :, :]).then_inc(s_pad, 16)
                sp.wait_ge(s_pad, 16 * (NE + 1) * (f + 1))

                def load(t, par):
                    row0 = sp.value_load(toff_i[0:1, f, bass.ds(t, 1)], min_val=0, max_val=NE * REG)
                    sp.dma_start(xt[:, par, :, :],
                                 rows_dram[f][bass.ds(row0, SLOT), :].rearrange("(p r) w -> p r w", r=2))\
                        .then_inc(s_xt[par], 16)

                for t in range(2):
                    if f > 0:
                        sp.wait_ge(s_t, f * NTILE + t - 1)
                        sp.wait_ge(s_meta, f * NTILE + t - 1)
                    load(t, t % 2)
                with sp.Fori(H0, H1) as h:
                    for par in range(2):
                        sp.wait_ge(s_t, 2 * h + (f * NTILE + par - 1))
                        sp.wait_ge(s_meta, 2 * h + (f * NTILE + par - 1))
                        load(2 * h + par, par)
                sp.wait_ge(s_t, f * NTILE + NTILE - 2)
                sp.wait_ge(s_meta, f * NTILE + NTILE - 2)
                load(NTILE - 1, 0)
                for par in range(BUFS):
                    sp.wait_ge(s_ysent[par], 32 * even_odd(f + 1, par, 0))
                for g in range(BATCH):
                    n = f * BATCH + g
                    if n >= 2:
                        sp.wait_ge(s_x1, n - 1)
                    for k in range(TOPK):
                        sp.dma_start(yin[:, n % 2, k, :, :],
                                     y_dram[f].rearrange("(k b t p) d -> k b p t d", k=TOPK, b=BATCH, p=P)[k, g])\
                            .then_inc(s_yin[n % 2], 16)
            for g in range(BATCH):
                sp.wait_ge(s_x1, BATCH + g + 1)
                sp.dma_start(out[g].rearrange("(t p) d -> p t d", p=P), xres[:, g, :, :]).then_inc(s_out, 16)
            sp.wait_ge(s_out, 16 * BATCH)

        @block.gpsimd
        def _(pool):
            pool.memset(ident[:, :], 0.0).then_inc(s_pool, 1)
            pool.memset(before[:, :], 1.0).then_inc(s_pool, 1)
            pool.iota(rev_i[:, 0:NE], pattern=[[-1, NE]], base=NE, channel_multiplier=0).then_inc(s_pool, 1)
            pool.iota(rev_i[:, NE:2 * NE], pattern=[[REG, NE]], base=0, channel_multiplier=0).then_inc(s_pool, 1)
            pool.iota(rev_i[:, 2 * NE:], pattern=[[1, NTILE]], base=0, channel_multiplier=0).then_inc(s_pool, 1)
            pool.iota(dest_i[:, :, :, :], pattern=[[TOK, TOPK], [SEQ, BATCH], [P, GT]], base=0,
                      channel_multiplier=1).then_inc(s_pool, 1)
            pool.wait_ge(s_pool, 2)
            pool.affine_select(out=ident[:, :], in_=ident[:, :], compare_op=ALU.not_equal, fill=1.0, base=0,
                               pattern=[[-1, P]], channel_multiplier=1).then_inc(s_pool, 1)
            pool.affine_select(out=before[:, :], in_=before[:, :], compare_op=ALU.is_gt, fill=0.0, base=0,
                               pattern=[[1, P]], channel_multiplier=-1).then_inc(s_pool, 1)
            pool.memset(ones16[:, :], 1.0).then_inc(s_pool, 1)

            def send_rows(f, g):
                pool.wait_ge(s_slot, f * BATCH + g + 1)
                for k in range(TOPK):
                    for t in range(GT):
                        pool.indirect_dma_start(
                            out=rows_dram[f], out_offset=bass.IndirectOffsetOnAxis(ap=slot_i[:, k, f, g, t:t + 1], axis=0),
                            in_=rows[:, k, g, t, :], in_offset=None).then_inc(s_sent, 16)

            last_row = pool.to_reg(TOPK * TOK - 1)

            def send_y(f, par, waitval):
                pool.wait_ge(s_yout, waitval)
                pool.sem_inc(s_ygo, 1)
                for r in range(2):
                    pool.indirect_dma_start(
                        out=y_dram[f],
                        out_offset=bass.IndirectOffsetOnAxis(ap=dest[:, par, r:r + 1], axis=0),
                        in_=yout[:, par, r, :], in_offset=None, bounds_check=last_row,
                        oob_is_err=False).then_inc(s_ysent[par], 16)

            for f in range(2):
                for kind, ff, g in (order[:first_middle] if f == 0 else order[first_middle:]):
                    if kind == "ffn":
                        send_rows(ff, g)
                b = f * NTILE
                for t in range(2):
                    send_y(f, t, b + t + 1)
                with pool.Fori(H0, H1) as h:
                    for par in range(2):
                        send_y(f, par, 2 * h + (b + par + 1))
                send_y(f, 0, b + NTILE)

        @block.scalar
        def _(act_e):
            def layernorm_std(n):
                act_e.wait_ge(s_var, n + 1)
                nc.scalar.activation(std[:, n % 2, :], mv[:, n % 2, :, 1], ACT.Sqrt,
                                     bias=eps_c[:, 0:1]).then_inc(s_std, 1)

            def transposed(n):
                if n >= 2:
                    kind, f, g = order[n - 2]
                    if kind == "ffn":
                        act_e.wait_ge(s_logit, f * BATCH + g + 1)
                    else:
                        act_e.wait_ge(s_cx, g + 1)
                for c in range(2):
                    act_e.wait_ge(s_tr, 2 * n + c + 1)
                    nc.scalar.copy(xnt[:, n % 2, c * HALF:(c + 1) * HALF], t_ps[c][:, :]).then_inc(s_xnt, 1)

            def high_part(f, g, n):
                act_e.wait_ge(s_xn, n + 1)
                if f > 0:
                    act_e.wait_ge(s_sent, 16 * TOPK * BATCH * GT)
                nc.scalar.copy(rows16[:, 0, g, :, 0:P], xn[:, n % 2, :, :]).then_inc(s_hi, 1)

            def exp_dif(f, g):
                q = f * BATCH + g
                act_e.wait_ge(s_dif, q + 1)
                nc.scalar.activation(edif[:, q % 2, :], dif[:, q % 2, :], ACT.Exp).then_inc(s_edif, 1)

            def instance(n):
                kind, f, g = order[n]
                layernorm_std(n)
                if kind == "ffn":
                    high_part(f, g, n)
                transposed(n)
                if kind == "ffn":
                    exp_dif(f, g)

            def weight_high(e):
                act_e.wait_ge(s_w[e % 2], 32 * (e // 2 + 1))
                nc.scalar.mul(w1h[:, e * 2 * HID:(e + 1) * 2 * HID], wst[:, e % 2, 0:2 * HID], WS).then_inc(s_wh, 1)
                nc.scalar.mul(w2h[:, e * HB * P:(e + 1) * HB * P], wst[:, e % 2, 2 * HID:], WS).then_inc(s_wh, 1)

            act_e.wait_ge(s_const, 1)
            for n in range(first_middle):
                instance(n)
            for e in range(NE):
                weight_high(e)
            act_e.wait_ge(s_small, 16 * 12)
            nc.scalar.activation(lam[:, 0:2], vec[:, 0:2], ACT.Exp).then_inc(s_lama, 1)
            nc.scalar.activation(lam[:, 2:3], vec[:, 3:4], ACT.Exp).then_inc(s_lama, 1)
            act_e.wait_ge(s_lama, 2)
            nc.scalar.activation(lam[:, 3:4], lam[:, 0:1], ACT.Exp, scale=-1.0).then_inc(s_lama, 1)
            act_e.wait_ge(s_lam, 1)
            nc.scalar.activation(lam[:, 5:6], lam[:, 4:5], ACT.Sin).then_inc(s_lama, 1)
            nc.scalar.activation(lam[:, 6:7], lam[:, 4:5], ACT.Sin, scale=0.5).then_inc(s_lama, 1)
            act_e.wait_ge(s_btr, 1)
            nc.scalar.copy(bt[:, :, :], t_ps[0][:, 0:2 * P].rearrange("p (a d) -> p a d", a=2)).then_inc(s_bt, 1)

            def gates(f, e_reg, j, ready):
                act_e.wait_ge(s_up, ready)
                nc.scalar.activation(gate[:, j, :], up_ps[j][:, 0:SLOT], ACT.Silu, scale=1.0 / WS,
                                     bias=b1g[:, bass.ds(e_reg, 1), j]).then_inc(s_gate, 1)

            def act_high(par, half, ready, free):
                act_e.wait_ge(s_act, ready)
                if free is not None:
                    act_e.wait_ge(s_down, free)
                nc.scalar.copy(acth[:, par, 2 * half:2 * half + 2, :],
                               act[:, 2 * half:2 * half + 2, :]).then_inc(s_acth, 1)

            def weighted(par, ready, sent):
                act_e.wait_ge(s_ysum, ready)
                if sent is not None:
                    act_e.wait_ge(s_ysent[par], sent)
                for r in range(2):
                    ins = nc.scalar.mul(yout[:, par, r, :], ysum[:, par, r, :],
                                        weight[:, par, r:r + 1])
                ins.then_inc(s_yout, 1)

            def step(f, s, par, lag, first):
                b = f * NTILE
                e_reg = act_e.value_load(tex_i[0:1, f, bass.ds(s, 1)], min_val=0, max_val=NE - 1)
                for half in range(2):
                    for j in (2 * half, 2 * half + 1):
                        gates(f, e_reg, j, s * HB + (b * HB + j + 1))
                    act_high(par, half, s * HB + (b * HB + 2 * half + 2),
                             None if first and f == 0 else s + (b - 1))
                    if half == 0 and not first:
                        weighted(par, s + (b - 1), lag)

            for f in range(2):
                if f > 0:
                    for n in range(first_middle, len(order)):
                        instance(n)
                act_e.wait_ge(s_tab, f + 1)
                for t in range(2):
                    step(f, t, t, None, True)
                with act_e.Fori(H0, H1) as h:
                    for par in range(2):
                        step(f, 2 * h + par, par, h * 32 + 32 * even_odd(f, par, -1), False)
                t = NTILE - 1
                step(f, t, 0, 32 * even_odd(f, 0, t // 2 - 1), False)
                for t in (NTILE - 2, NTILE - 1):
                    weighted(t % 2, f * NTILE + t + 1, 32 * even_odd(f, t % 2, t // 2))

        @block.vector
        def _(dve):
            count = [0]

            def link(ins):
                count[0] += 1
                ins.then_inc(s_chain, 1)
                dve.wait_ge(s_chain, count[0])

            V = nc.vector

            def over_e(a):
                return a.unsqueeze(2).to_broadcast([P, GT, NE])

            def over_t(a):
                return a.unsqueeze(1).to_broadcast([P, GT, NE])

            V.memset(eps_c[:, :], EPS).then_inc(s_const, 1)
            V.memset(ones8[:, :], 1.0)
            V.memset(seen[:, :, 0, :], 0.0)
            link(V.memset(padrow[:, :, :], 0.0))
            link(V.memset(padrow[:, :, P:P + 1], float(OUTSIDE)))
            dve.wait_ge(s_pool, 9)
            V.tensor_copy(ident16[:, :], ident[:, :]).then_inc(s_const, 1)
            link(V.tensor_copy(rev_f[:, :], rev_i[:, :]))
            for k in range(TOPK):
                for g in range(BATCH):
                    ins = V.tensor_copy(rows[:, k, g, :, P:P + 1],
                                        dest_i[:, k, g, :].unsqueeze(2))
            link(ins)

            def normalise(n):
                kind, f, g = order[n]
                for t in range(GT):
                    ins = V.bn_stats(bn[:, t, :], xres[:, g, t, :])
                link(ins)
                if n >= 2:
                    dve.wait_ge(s_std, n - 1)
                for t in range(GT):
                    ins = V.bn_aggr(mv[:, n % 2, t, :], bn[:, t, :])
                ins.then_inc(s_var, 1)
                dve.wait_ge(s_std, n + 1)
                link(V.reciprocal(rstd[:, n % 2, :], std[:, n % 2, :]))
                if n >= 2:
                    dve.wait_ge(s_tr, 2 * (n - 1))
                    kind2, f2, g2 = order[n - 2]
                    if kind2 == "ffn":
                        dve.wait_ge(s_hi, f2 * BATCH + g2 + 1)
                for t in range(GT):
                    ins = V.tensor_scalar(xn[:, n % 2, t, :], xres[:, g, t, :], mv[:, n % 2, t, 0:1],
                                          rstd[:, n % 2, t:t + 1], ALU.subtract, ALU.mult)
                ins.then_inc(s_xn, 1)

            def row_parts(f, g, n):
                dve.wait_ge(s_hi, f * BATCH + g + 1)
                link(V.tensor_tensor(rows16[:, 0, g, :, P:2 * P], xn[:, n % 2, :, :], rows16[:, 0, g, :, 0:P],
                                     ALU.subtract))
                link(V.tensor_copy(rows16[:, 1, g, :, :], rows16[:, 0, g, :, :]))

            def pick(o, m):
                link(V.tensor_reduce(m[:, :], lg[:, :, :], AX, ALU.max))
                link(V.tensor_tensor(tmp8[:, :, :], lg[:, :, :], over_e(m[:, :]), ALU.is_ge))
                link(V.tensor_tensor(tmp8[:, :, :], tmp8[:, :, :], over_t(rev_f[:, 0:NE]), ALU.mult))
                link(V.tensor_reduce(rr[:, :], tmp8[:, :, :], AX, ALU.max))
                link(V.tensor_tensor(o[:, :, :], tmp8[:, :, :], over_e(rr[:, :]), ALU.is_equal))

            def route(f, g):
                q = f * BATCH + g
                dve.wait_ge(s_logit, q + 1)
                link(V.tensor_tensor(lg[:, :, :], logit_ps[:, 0:GT * NE].rearrange("p (t e) -> p t e", e=NE),
                                     over_t(rbb[:, :]), ALU.add))
                pick(oh1, m1)
                link(V.scalar_tensor_tensor(lg[:, :, :].rearrange("p t e -> p (t e)"),
                                            oh1[:, :, :].rearrange("p t e -> p (t e)"), -BIG,
                                            lg[:, :, :].rearrange("p t e -> p (t e)"), ALU.mult, ALU.add))
                pick(oh2, m2)
                V.tensor_tensor(dif[:, q % 2, :], m2[:, :], m1[:, :], ALU.subtract).then_inc(s_dif, 1)
                V.tensor_tensor(oh[:, q % 2, :, :], oh1[:, :, :], oh2[:, :, :], ALU.add).then_inc(s_oh, 1)
                dve.wait_ge(s_oh, q + 1)
                link(V.tensor_reduce(seen1[:, :], oh[:, q % 2, :, :].rearrange("p t e -> p e t"), AX, ALU.add))
                V.tensor_tensor(seen[:, f, g + 1, :], seen[:, f, g, :], seen1[:, :], ALU.add).then_inc(s_lg, 1)
                dve.wait_ge(s_edif, q + 1)
                link(V.tensor_scalar(den[:, :], edif[:, q % 2, :], 1.0, 2.0 * WS * WS, ALU.add, ALU.mult))
                link(V.reciprocal(wk[:, 0, :], den[:, :]))
                link(V.tensor_tensor(wk[:, 1, :], wk[:, 0, :], edif[:, q % 2, :], ALU.mult))
                for k in range(TOPK):
                    link(V.tensor_copy(rows[:, k, g, :, P + 1:P + 2], wk[:, k, :].unsqueeze(2)))
                dve.wait_ge(s_rank, q + 1)
                link(V.tensor_tensor(slotf[:, :, :], rank_ps[:, 0:GT * NE].rearrange("p (t e) -> p t e", e=NE),
                                     over_t(rev_f[:, NE:2 * NE]), ALU.add))
                for k, o in enumerate((oh1, oh2)):
                    link(V.tensor_tensor(tmp8[:, :, :], slotf[:, :, :], o[:, :, :], ALU.mult))
                    link(V.tensor_reduce(slot1[:, :], tmp8[:, :, :], AX, ALU.add))
                    ins = V.tensor_copy(slot_i[:, k, f, g, :], slot1[:, :])
                    if k == 0:
                        link(ins)
                ins.then_inc(s_slot, 1)

            def tile_table(f):
                dve.wait_ge(s_cnt, f + 1)
                link(V.tensor_copy(cnt[:, :], rank_ps[:, 128:128 + NE]))
                link(V.tensor_scalar(cnt_i[:, :], cnt[:, :], float(SLOT - 1), None, ALU.add))
                link(V.tensor_scalar(cnt_i[:, :], cnt_i[:, :], SLOT.bit_length() - 1, None, ALU.logical_shift_right))
                link(V.tensor_copy(ntile[:, :], cnt_i[:, :]))
                link(V.tensor_tensor_scan(upto[:, :], ones8[:, :], ntile[:, :], 0.0, ALU.mult, ALU.add))
                link(V.tensor_tensor(pad_i[:, f, :], cnt[:, :], rev_f[:, NE:2 * NE], ALU.add))
                tiles = rev_f[:, 2 * NE:]

                def grid(a):
                    return a.unsqueeze(1).to_broadcast([P, NTILE, NE])

                link(V.tensor_tensor(ge_hi[:, :, :], tiles.unsqueeze(2).to_broadcast([P, NTILE, NE]),
                                     grid(upto[:, :]), ALU.is_ge))
                link(V.tensor_reduce(tex[:, :], ge_hi[:, :, :], AX, ALU.add))
                link(V.tensor_tensor(ntile[:, :], upto[:, :], ntile[:, :], ALU.subtract))
                link(V.tensor_tensor(ge_lo[:, :, :], tiles.unsqueeze(2).to_broadcast([P, NTILE, NE]),
                                     grid(ntile[:, :]), ALU.is_ge))
                link(V.tensor_tensor(ge_lo[:, :, :], ge_lo[:, :, :], ge_hi[:, :, :], ALU.subtract))
                link(V.scalar_tensor_tensor(base8[:, :], ntile[:, :], -float(SLOT), rev_f[:, NE:2 * NE],
                                            ALU.mult, ALU.add))
                link(V.tensor_tensor(ge_lo[:, :, :], ge_lo[:, :, :], grid(base8[:, :]), ALU.mult))
                link(V.tensor_reduce(toff[:, :], ge_lo[:, :, :], AX, ALU.add))
                link(V.scalar_tensor_tensor(toff[:, :], tiles, float(SLOT), toff[:, :], ALU.mult, ALU.add))
                link(V.tensor_scalar(slotf[:, 0, :], upto[:, :], 0.0, None, ALU.add))
                unused = ge_hi[:, :, NE - 1]
                link(V.scalar_tensor_tensor(ge_lo[:, :, 0], tiles, -float(SLOT), unused, ALU.mult, ALU.mult))
                link(V.scalar_tensor_tensor(ge_lo[:, :, 0], unused, float(NE * REG), ge_lo[:, :, 0],
                                            ALU.mult, ALU.add))
                link(V.tensor_tensor(toff_i[:, f, :], toff[:, :], ge_lo[:, :, 0], ALU.add))
                V.tensor_scalar(tex_i[:, f, :], tex[:, :], float(NE - 1), None, ALU.min).then_inc(s_tab, 1)
                dve.wait_ge(s_tab, f + 1)

            def weight_low(e):
                for i, (hi, lo, a, b) in enumerate(((w1h, w1l, 0, 2 * HID), (w2h, w2l, 2 * HID, 2 * HID + HB * P))):
                    w = b - a
                    dve.wait_ge(s_wh, 2 * e + i + 1)
                    V.scalar_tensor_tensor(lo[:, e * w:(e + 1) * w], wst[:, e % 2, a:b], WS, hi[:, e * w:(e + 1) * w],
                                           ALU.mult, ALU.subtract).then_inc(s_wl, 1)

            def lru_constants():
                dve.wait_ge(s_lama, 2)
                link(V.tensor_scalar(lam_i[:, :], lam[:, 1:2], 1.0 / TWO_PI, None, ALU.mult))
                link(V.tensor_copy(lam[:, 7:8], lam_i[:, :]))
                link(V.scalar_tensor_tensor(lam[:, 8:9], lam[:, 7:8], -6.28125, lam[:, 1:2], ALU.mult, ALU.add))
                link(V.scalar_tensor_tensor(lam[:, 8:9], lam[:, 7:8], -(TWO_PI - 6.28125), lam[:, 8:9],
                                            ALU.mult, ALU.add))
                V.tensor_scalar(lam[:, 4:5], lam[:, 8:9], -PI, PI, ALU.max, ALU.min).then_inc(s_lam, 1)
                for i in range(2):
                    ins = V.tensor_scalar(bst[:, i, :], bst[:, i, :], lam[:, 2:3], None, ALU.mult)
                ins.then_inc(s_bsc, 1)
                link(V.tensor_scalar(diag_d[:, :], ident[:, :], vec[:, 2:3], None, ALU.mult))
                link(V.tensor_scalar(nct_re[:, :], ct_re[:, :], -1.0, None, ALU.mult))
                link(V.tensor_scalar(nct_im[:, :], ct_im[:, :], -1.0, None, ALU.mult))
                dve.wait_ge(s_lama, 5)
                link(V.tensor_tensor(lam[:, 9:10], lam[:, 6:7], lam[:, 6:7], ALU.mult))
                link(V.tensor_scalar(lam[:, 9:10], lam[:, 9:10], -2.0, 1.0, ALU.mult, ALU.add))

                def unit_modulus():
                    link(V.tensor_tensor(lam[:, 11:12], lam[:, 9:10], lam[:, 9:10], ALU.mult))
                    link(V.scalar_tensor_tensor(lam[:, 12:13], lam[:, 10:11], lam[:, 10:11], lam[:, 11:12],
                                                ALU.mult, ALU.add))
                    link(V.tensor_scalar(lam[:, 12:13], lam[:, 12:13], -0.5, 1.5, ALU.mult, ALU.add))
                    link(V.tensor_scalar(lam[:, 9:11], lam[:, 9:11], lam[:, 12:13], None, ALU.mult))

                link(V.tensor_copy(lam[:, 10:11], lam[:, 5:6]))
                unit_modulus()
                V.memset(ctab[:, 0:1], 1.0)
                link(V.memset(stab[:, 0:1], 0.0))
                n = 1
                while n < SEQ:
                    V.tensor_scalar(prod[:, 0, 0:n], stab[:, 0:n], lam[:, 10:11], None, ALU.mult)
                    link(V.tensor_scalar(prod[:, 1, 0:n], ctab[:, 0:n], lam[:, 10:11], None, ALU.mult))
                    V.scalar_tensor_tensor(ctab[:, n:2 * n], ctab[:, 0:n], lam[:, 9:10], prod[:, 0, 0:n],
                                           ALU.mult, ALU.subtract)
                    link(V.scalar_tensor_tensor(stab[:, n:2 * n], stab[:, 0:n], lam[:, 9:10], prod[:, 1, 0:n],
                                                ALU.mult, ALU.add))
                    n *= 2
                    if n < SEQ:
                        link(V.tensor_tensor(lam[:, 13:14], lam[:, 10:11], lam[:, 10:11], ALU.mult))
                        link(V.tensor_tensor(lam[:, 14:15], lam[:, 9:10], lam[:, 10:11], ALU.mult))
                        link(V.scalar_tensor_tensor(lam[:, 9:10], lam[:, 9:10], lam[:, 9:10], lam[:, 13:14],
                                                    ALU.mult, ALU.subtract))
                        link(V.tensor_scalar(lam[:, 10:11], lam[:, 14:15], 2.0, None, ALU.mult))
                        unit_modulus()

            def add_outputs(f, g):
                n = f * BATCH + g
                dve.wait_ge(s_yin[n % 2], 16 * TOPK * (n // 2 + 1))
                link(V.tensor_tensor(xres[:, g, :, :], xres[:, g, :, :], yin[:, n % 2, 0, :, :], ALU.add))
                V.tensor_tensor(xres[:, g, :, :], xres[:, g, :, :], yin[:, n % 2, 1, :, :], ALU.add).then_inc(s_x1, 1)
                dve.wait_ge(s_x1, n + 1)

            def recurrence(g):
                for c in range(2):
                    cols = slice(c * HALF, (c + 1) * HALF)
                    dve.wait_ge(s_bu, 2 * g + c + 1)
                    re, im = up_ps[0][:, :], up_ps[1][:, :]
                    V.tensor_tensor(rot[0][:, :], ctab[:, cols], re, ALU.mult)
                    V.tensor_tensor(rot[1][:, :], stab[:, cols], im, ALU.mult)
                    V.tensor_tensor(rot[2][:, :], ctab[:, cols], im, ALU.mult)
                    ins = V.tensor_tensor(rot[3][:, :], stab[:, cols], re, ALU.mult)
                    ins.then_inc(s_bud, 1)
                    dve.wait_ge(s_bud, 2 * g + c + 1)
                    V.tensor_tensor(rot[0][:, :], rot[0][:, :], rot[1][:, :], ALU.add)
                    link(V.tensor_tensor(rot[2][:, :], rot[2][:, :], rot[3][:, :], ALU.subtract))
                    decay = lam[:, 3:4].to_broadcast([P, HALF])
                    for y, v in ((yre, rot[0]), (yim, rot[2])):
                        start = 0.0 if c == 0 else y[:, HALF - 1:HALF]
                        ins = V.tensor_tensor_scan(y[:, cols], decay, v[:, :], start, ALU.mult, ALU.add)
                    link(ins)
                if g > 0:
                    dve.wait_ge(s_cx, g)
                for i, (y, tab) in enumerate(((yre, ctab), (yim, stab), (yre, stab), (yim, ctab))):
                    ins = V.tensor_tensor(prod[:, i, :], y[:, :], tab[:, :], ALU.mult)
                ins.then_inc(s_prod, 1)

            def add_recurrence(g):
                dve.wait_ge(s_cx, g + 1)
                for c in range(2):
                    sl = xres[:, g, 4 * c:4 * c + 4, :].rearrange("p t d -> p (t d)")
                    ins = V.tensor_tensor(sl, sl, y_ps[c][:, :], ALU.add)
                ins.then_inc(s_x2, 1)
                dve.wait_ge(s_x2, g + 1)

            for n in range(first_middle):
                g = order[n][2]
                dve.wait_ge(s_xin[g], 16)
                if n == 0:
                    dve.wait_ge(s_small, 16 * 12)
                normalise(n)
                row_parts(0, g, n)
                route(0, g)
            tile_table(0)
            V.tensor_scalar(b1u[:, :].rearrange("p (e j) -> p e j", e=NE), b1g[:, :, HB:2 * HB], WS, None, ALU.mult)
            link(V.tensor_scalar(b2b[:, :], b2b[:, :], WS * WS, None, ALU.mult))
            for e in range(NE):
                weight_low(e)
            lru_constants()

            def take_tile(f, t, par, b):
                dve.wait_ge(s_t, t + (b + 1))
                V.tensor_copy(xt_t[:, par, :, :].rearrange("p a s -> p (a s)"), t16[par][:, 0:512]).then_inc(s_xtt, 1)
                V.tensor_copy(meta[:, bass.ds(t, 1), :, :], xt[:, par, :, P:].unsqueeze(1)).then_inc(s_meta, 1)

            def activate(e_reg, j, ready):
                dve.wait_ge(s_gate, ready)
                V.scalar_tensor_tensor(act[:, j, :], up_ps[j][:, SLOT:], b1u[:, bass.ds(e_reg * HB + j, 1)],
                                       gate[:, j, :], ALU.add, ALU.mult).then_inc(s_act, 1)

            def act_low(par, half, ready):
                dve.wait_ge(s_acth, ready)
                h2 = slice(2 * half, 2 * half + 2)
                V.tensor_tensor(actl[:, par, h2, :], act[:, h2, :], acth[:, par, h2, :],
                                ALU.subtract).then_inc(s_actl, 1)

            def out_bias(f, t, par, b, sent):
                e_reg = dve.value_load(tex_i[0:1, f, bass.ds(t, 1)], min_val=0, max_val=NE - 1)
                dve.wait_ge(s_meta, t + (b + 1))
                if sent is not None:
                    dve.wait_ge(s_ysent[par], sent)
                V.tensor_copy(dest[:, par, :].unsqueeze(1), meta[:, bass.ds(t, 1), :, 0])
                V.tensor_copy(weight[:, par, :].unsqueeze(1), meta[:, bass.ds(t, 1), :, 1])
                dve.wait_ge(s_down, t + (b + 1))
                V.tensor_tensor(ysum[:, par, :, :], y_ps[par][:, 0:2 * P].rearrange("p (r d) -> p r d", r=2),
                                b2b[:, bass.ds(e_reg * P, P)].unsqueeze(1).to_broadcast([P, 2, P]),
                                ALU.add).then_inc(s_ysum, 1)

            def step(f, s, par, sent, first, last):
                b = f * NTILE
                e_reg = dve.value_load(tex_i[0:1, f, bass.ds(s, 1)], min_val=0, max_val=NE - 1)
                for j in (0, 1):
                    activate(e_reg, j, s * HB + (b * HB + j + 1))
                if not first:
                    out_bias(f, s - 2, par, b, sent)
                act_low(par, 0, 2 * s + (2 * b + 1))
                for j in (2, 3):
                    activate(e_reg, j, s * HB + (b * HB + j + 1))
                if not last:
                    take_tile(f, s + 1, 1 - par, b)
                act_low(par, 1, 2 * s + (2 * b + 2))

            for f in range(2):
                if f > 0:
                    for n in range(first_middle, len(order)):
                        kind, ff, g = order[n]
                        if kind == "lru":
                            add_outputs(0, g)
                            normalise(n)
                            recurrence(g)
                        else:
                            add_recurrence(g)
                            normalise(n)
                            row_parts(1, g, n)
                            route(1, g)
                    tile_table(1)
                take_tile(f, 0, 0, f * NTILE)
                step(f, 0, 0, None, True, False)
                step(f, 1, 1, None, True, False)
                with dve.Fori(H0, H1) as h:
                    for par in range(2):
                        step(f, 2 * h + par, par, h * 32 + 32 * even_odd(f, par, -1), False, False)
                t = NTILE - 1
                step(f, t, 0, 32 * even_odd(f, 0, t // 2 - 1), False, True)
                for t in (NTILE - 2, NTILE - 1):
                    out_bias(f, t, t % 2, f * NTILE, 32 * even_odd(f, t % 2, t // 2))
            for g in range(BATCH):
                add_outputs(1, g)

        @block.tensor
        def _(pe):
            T = nc.tensor

            def transpose_rows(n):
                pe.wait_ge(s_xn, n + 1)
                for c in range(2):
                    if n >= 1:
                        pe.wait_ge(s_xnt, 2 * (n - 1) + c + 1)
                    for j in range(4):
                        ins = T.transpose(t_ps[c][:, j * P:(j + 1) * P], xn[:, n % 2, 4 * c + j, :], ident[:, :])
                    ins.then_inc(s_tr, 1)

            def logits_and_ranks(f, g, n):
                q = f * BATCH + g
                pe.wait_ge(s_xnt, 2 * n + 2)
                if q >= 1:
                    pe.wait_ge(s_slot, q)
                for t in range(GT):
                    ins = T.matmul(logit_ps[:, t * NE:(t + 1) * NE], xnt[:, n % 2, t * P:(t + 1) * P], rwt[:, :],
                                   start=True, stop=True)
                ins.then_inc(s_logit, 1)
                pe.wait_ge(s_oh, q + 1)
                ranks = rank_ps[:, 0:GT * NE].rearrange("p (t e) -> p t e", e=NE)
                T.matmul(ranks, before[:, :], oh[:, q % 2, :, :], start=True, stop=False)
                for t in range(GT - 1):
                    m = GT - 1 - t
                    T.matmul(ranks[:, t + 1:, :], ones16[:, :],
                             oh[:, q % 2, t, :].unsqueeze(1).to_broadcast([P, m, NE]), start=False, stop=False)
                T.matmul(ranks, ones16[:, :], seen[:, f, g, :].unsqueeze(1).to_broadcast([P, GT, NE]),
                         start=False, stop=True).then_inc(s_rank, 1)
                if g == BATCH - 1:
                    pe.wait_ge(s_lg, q + 1)
                    pe.wait_ge(s_slot, q + 1)
                    T.matmul(rank_ps[:, 128:128 + NE], ones16[:, :], seen[:, f, BATCH, :],
                             start=True, stop=True).then_inc(s_cnt, 1)

            pe.wait_ge(s_const, 2)
            for n in range(first_middle):
                transpose_rows(n)
                logits_and_ranks(0, order[n][2], n)
            pe.wait_ge(s_bsc, 1)
            pe.wait_ge(s_xnt, 2 * first_middle)
            for i in range(2):
                ins = T.transpose(t_ps[0][:, i * P:(i + 1) * P], bst[:, i, :], ident[:, :])
            ins.then_inc(s_btr, 1)

            def bu(g, n):
                for c in range(2):
                    pe.wait_ge(s_xnt, 2 * n + c + 1)
                    if 2 * g + c > 0:
                        pe.wait_ge(s_bud, 2 * g + c)
                    for i in range(2):
                        ins = T.matmul(up_ps[i][:, :], bt[:, i, :], xnt[:, n % 2, c * HALF:(c + 1) * HALF],
                                       start=True, stop=True)
                    ins.then_inc(s_bu, 1)

            def cx(g, n):
                pe.wait_ge(s_prod, g + 1)
                if g > 0:
                    pe.wait_ge(s_x2, g)
                for t in range(GT):
                    cols = slice(t * P, (t + 1) * P)
                    o = y_ps[t // 4][:, (t % 4) * P:(t % 4 + 1) * P]
                    terms = [(prod[:, 0, cols], ct_re), (prod[:, 1, cols], nct_re), (prod[:, 2, cols], nct_im),
                             (prod[:, 3, cols], nct_im), (xnt[:, n % 2, cols], diag_d)]
                    for i, (a, m) in enumerate(terms):
                        ins = T.matmul(o, a, m[:, :], start=(i == 0), stop=(i == len(terms) - 1))
                ins.then_inc(s_cx, 1)

            def transpose_tile(t, par, b, landed, free):
                pe.wait_ge(s_xt[par], landed)
                if free is not None:
                    pe.wait_ge(s_xtt, free)
                for a in range(2):
                    for r in range(2):
                        ins = T.transpose(t16[par][:, (2 * a + r) * P:(2 * a + r + 1) * P],
                                          xt16[:, par, r, a * P:(a + 1) * P], ident16[:, :])
                ins.then_inc(s_t, 1)

            def up(f, s, par, b, first):
                e_reg = pe.value_load(tex_i[0:1, f, bass.ds(s, 1)], min_val=0, max_val=NE - 1)
                pe.wait_ge(s_xtt, s + (b + 1))
                for j in range(HB):
                    if not first:
                        pe.wait_ge(s_act, s * HB + ((b - 1) * HB + j + 1))
                    for half in range(2):
                        o = up_ps[j][:, half * SLOT:(half + 1) * SLOT]
                        at = e_reg * (2 * HID) + (half * HID + j * P)
                        T.matmul(o, w1h[:, bass.ds(at, P)], xt_t[:, par, 0, :], start=True, stop=False)
                        T.matmul(o, w1h[:, bass.ds(at, P)], xt_t[:, par, 1, :], start=False, stop=False)
                        ins = T.matmul(o, w1l[:, bass.ds(at, P)], xt_t[:, par, 0, :], start=False, stop=True)
                    ins.then_inc(s_up, 1)

            def down(f, s, par, b, first):
                e_reg = pe.value_load(tex_i[0:1, f, bass.ds(s, 1)], min_val=0, max_val=NE - 1)
                pe.wait_ge(s_actl, 2 * s + (2 * b + 2))
                if not first:
                    pe.wait_ge(s_ysum, s + (b - 1))
                for r in range(2):
                    o = y_ps[par][:, r * P:(r + 1) * P]
                    rs = slice(r * P, (r + 1) * P)
                    for c in range(HB):
                        at = e_reg * (HB * P) + c * P
                        T.matmul(o, acth[:, par, c, rs], w2h[:, bass.ds(at, P)], start=(c == 0), stop=False)
                        T.matmul(o, acth[:, par, c, rs], w2l[:, bass.ds(at, P)], start=False, stop=False)
                        ins = T.matmul(o, actl[:, par, c, rs], w2h[:, bass.ds(at, P)], start=False,
                                       stop=(c == HB - 1))
                ins.then_inc(s_down, 1)

            for f in range(2):
                b = f * NTILE
                if f > 0:
                    inst = {order[n]: n for n in range(first_middle, len(order))}
                    for n in range(first_middle, len(order)):
                        kind, ff, g = order[n]
                        transpose_rows(n)
                        if kind == "lru":
                            bu(g, n)
                            cx(g, n)
                        else:
                            logits_and_ranks(1, g, n)
                else:
                    pe.wait_ge(s_wl, 2 * NE)
                pe.wait_ge(s_tab, f + 1)
                if f == 0:
                    pe.wait_ge(s_bt, 1)
                transpose_tile(0, 0, b, 16 * (even_odd(f, 0, 0) + 1), None)
                up(f, 0, 0, b, True)
                transpose_tile(1, 1, b, 16 * (even_odd(f, 1, 0) + 1), None)
                up(f, 1, 1, b, False)
                transpose_tile(2, 0, b, 16 * (even_odd(f, 0, 1) + 1), b + 1)
                down(f, 0, 0, b, f == 0)
                with pe.Fori(H0, H1) as h:
                    for par in range(2):
                        s = 2 * h + par
                        up(f, s, par, b, False)
                        transpose_tile(s + 1, 1 - par, b, h * 16 + 16 * (even_odd(f, 1 - par, par) + 1), s + b)
                        down(f, s - 1, 1 - par, b, False)
                t = NTILE - 1
                up(f, t, 0, b, False)
                down(f, t - 1, 1, b, False)
                down(f, t, 0, b, False)


def _laid_out(inputs):
    import numpy as np
    a = {k.replace("L0_", ""): np.asarray(v) for k, v in inputs.items()}
    col = lambda v: v.reshape(P, 1)
    row = lambda v: v.reshape(-1)
    return [
        ("x", a["attn_inputs"]), ("nu_log", col(a["attn_nu_log"])), ("theta_log", col(a["attn_theta_log"])),
        ("b_re", a["attn_B_re"]), ("b_im", a["attn_B_im"]),
        ("c_re_t", a["attn_C_re"].T), ("c_im_t", a["attn_C_im"].T),
        ("d_vec", col(a["attn_D"])), ("gamma_log", col(a["attn_gamma_log"])),
        ("router_t", a["ffn_router_w"].T), ("router_b", row(a["ffn_router_b"])),
        ("w1_t", a["ffn_w1"].transpose(2, 0, 1)),
        ("b1_t", a["ffn_b1"].reshape(NE, 2 * HB, P).transpose(2, 0, 1)),
        ("w2_t", a["ffn_w2"].reshape(NE, P, HB, P).transpose(3, 0, 2, 1).reshape(P, NE, HB * P)),
        ("b2", row(a["ffn_b2"])),
    ]


def kernel(**inputs):
    import numpy as np
    import concourse.bacc as bacc
    from concourse import mybir as mb
    from concourse.bass_utils import run_bass_kernel_spmd

    nc = bacc.Bacc("TRN2", target_bir_lowering=False, num_devices=1)
    arrays, args = {}, []
    for name, a in _laid_out(inputs):
        a = np.ascontiguousarray(a)
        arrays[f"in_{name}"] = a
        args.append(nc.dram_tensor(f"in_{name}", a.shape, mb.dt.from_np(a.dtype), kind="ExternalInput").ap())
    args.append(nc.dram_tensor("out_0", (BATCH, SEQ, P), mb.dt.float32, kind="ExternalOutput").ap())
    macaron_block(nc, *args)
    result = run_bass_kernel_spmd(nc, [arrays], core_ids=[0])
    return result.results[0]["out_0"]
```

```python
from contextlib import ExitStack

import concourse.bass as bass
from concourse import mybir

FP32 = mybir.dt.float32
FP16 = mybir.dt.float16
I32 = mybir.dt.int32
ACT = mybir.ActivationFunctionType
ALU = mybir.AluOpType
AX = mybir.AxisListType.X

P = 128
BATCH, SEQ = 4, 1024
TOK = BATCH * SEQ
GT = SEQ // P
NE, HID, TOPK = 8, 512, 2
HB = HID // P
SLOT = 256
NTILE = TOPK * TOK // SLOT + NE - 1
REG = TOK + SLOT
ROWW = P + 2
WS = 16.0
OUTSIDE = 1 << 20
BIG = 3.0e38
TWO_PI = 6.283185307179586
PI = 3.14159274
LOG2_E, LN2_HIGH, LN2_LOW = 1.4426950408889634, 0.693359375, -2.12194440e-4
TWO_PI_PARTS = (6.28125, 0.0019350051879882812, 3.0199159819e-7)
EPS = 1e-5
BUFS = 2
STEP = 4
PEEL = 6
H0, H1 = 1, 1 + (NTILE - PEEL) // STEP
REST = PEEL + (H1 - H0) * STEP
HALF = SEQ // 2
TURNS = SEQ.bit_length() - 1


def macaron_block(nc, x, nu_log, theta_log, b_re, b_im, c_re_t, c_im_t, d_vec, gamma_log,
                  router_t, router_b, w1_t, b1_t, w2_t, b2, out):
    ctx = ExitStack()
    with ctx:
        def sb(name, shape, dt=FP32):
            return ctx.enter_context(nc.sbuf_tensor(name, shape, dt))

        def sem(name):
            return ctx.enter_context(nc.semaphore(name))

        rows_dram = [nc.dram_tensor(f"rows{f}", [NE * REG + SLOT, ROWW], FP32, kind="Internal").ap() for f in range(2)]
        y_dram = [nc.dram_tensor(f"y{f}", [TOPK * TOK, P], FP32, kind="Internal").ap() for f in range(2)]

        xres = sb("xres", [P, BATCH, GT, P])
        yin = sb("yin", [P, 2, TOPK, GT, P])
        xn = sb("xn", [P, 2, GT, P])
        xnt = sb("xnt", [P, 3, SEQ])
        rows = sb("rows", [P, TOPK, BATCH, GT, ROWW])
        bn = sb("bn", [P, GT, 6])
        mv = sb("mv", [P, 2, GT, 2])
        newton = sb("newton", [P, 3, GT])
        guess_i = sb("guess_i", [P, GT], I32)
        rstd = sb("rstd", [P, 2, GT])
        shift = sb("shift", [P, 2, GT])
        ident = sb("ident", [P, P])
        ident16 = sb("ident16", [P, P], FP16)
        before = sb("before", [P, P], FP16)
        ones16 = sb("ones16", [P, P], FP16)
        w1h = sb("w1h", [P, NE * 2 * HID], FP16)
        w1l = sb("w1l", [P, NE * 2 * HID], FP16)
        w2h = sb("w2h", [P, NE * HB * P], FP16)
        w2l = sb("w2l", [P, NE * HB * P], FP16)
        wst = sb("wst", [P, 2, 2 * HID + HB * P])
        b1g = sb("b1g", [P, NE, 2 * HB])
        bias = sb("bias", [P, STEP, 2 * HB])
        b2p = sb("b2p", [2, NE * P], FP16)
        rwt = sb("rwt", [P, NE])
        rbb = sb("rbb", [P, NE])
        rev_i = sb("rev_i", [P, 2 * NE + NTILE], I32)
        rev_f = sb("rev_f", [P, 2 * NE + NTILE])
        dest_i = sb("dest_i", [P, TOPK, BATCH, GT], I32)
        lg = sb("lg", [P, GT, NE])
        m1 = sb("m1", [P, GT])
        m2 = sb("m2", [P, GT])
        rr = sb("rr", [P, GT])
        oh1 = sb("oh1", [P, GT, NE])
        oh2 = sb("oh2", [P, GT, NE])
        tmp8 = sb("tmp8", [P, GT, NE])
        oh = sb("oh", [P, 2, GT, NE], FP16)
        seen = sb("seen", [P, 2, BATCH + 1, NE], FP16)
        seen1 = sb("seen1", [P, NE])
        dif = sb("dif", [P, 2, GT])
        edif = sb("edif", [P, 2, GT])
        den = sb("den", [P, GT])
        wk = sb("wk", [P, TOPK, GT])
        slotf = sb("slotf", [P, GT, NE])
        slot1 = sb("slot1", [P, GT])
        slot_i = sb("slot_i", [P, TOPK, 2, BATCH, GT], I32)
        cnt = sb("cnt", [P, NE])
        cnt_i = sb("cnt_i", [P, NE], I32)
        ntile = sb("ntile", [P, NE])
        upto = sb("upto", [P, NE])
        ones8 = sb("ones8", [P, NE])
        base8 = sb("base8", [P, NE])
        toff = sb("toff", [P, NTILE])
        tex = sb("tex", [P, NTILE])
        toff_i = sb("toff_i", [P, 2, NTILE], I32)
        tex_i = sb("tex_i", [P, 2, NTILE], I32)
        pad_i = sb("pad_i", [P, 2, NE], I32)
        padrow = sb("padrow", [P, 2, ROWW])
        xt = sb("xt", [P, STEP, 2, ROWW])
        dest = sb("dest", [P, STEP, 2], I32)
        weight = sb("weight", [P, STEP, 2])
        xt_t = sb("xt_t", [P, BUFS, 2, SLOT], FP16)
        gate = sb("gate", [P, HB, SLOT])
        act = sb("act", [P, HB, SLOT])
        yout = sb("yout", [P, STEP, 2, P])
        bst = sb("bst", [P, 2, P])
        bt = sb("bt", [P, 2, P])
        ct_re = sb("ct_re", [P, P])
        ct_im = sb("ct_im", [P, P])
        nct_im = sb("nct_im", [P, P])
        nct_re = sb("nct_re", [P, P])
        diag_d = sb("diag_d", [P, P])
        vec = sb("vec", [P, 4])
        lam = sb("lam", [P, 4])
        double = sb("double", [P, TURNS])
        trig = sb("trig", [P, 8, TURNS])
        turns_i = sb("turns_i", [P, TURNS], I32)
        ex = sb("ex", [P, 3, 4])
        ex_i = sb("ex_i", [P, 2, 4], I32)
        ctab = sb("ctab", [P, SEQ])
        stab = sb("stab", [P, SEQ])
        b2b = yin[0:2, 0, :, :, :].rearrange("p k t d -> p k (t d)")
        b2h = yin[0:2, 1, :, :, :].rearrange("p k t d -> p k (t d)").bitcast(FP16)
        ge_hi, ge_lo = [b[:, :, :].rearrange("p j s -> p (j s)")[:, 0:NTILE * NE].rearrange("p (t e) -> p t e", e=NE)
                        for b in (gate, act)]
        rot = [half[:, 2 * i:2 * i + 2, :].rearrange("p j s -> p (j s)") for half in (gate, act) for i in range(2)]
        yre, yim = wst[:, 0, 0:SEQ], wst[:, 1, 0:SEQ]
        prod = sb("prod", [P, 4, SEQ])
        acth, actl = [prod[:, i, :].bitcast(FP16).rearrange("p (b j s) -> p b j s", b=BUFS, j=HB) for i in range(2)]

        bank = [ctx.enter_context(nc.psum_tensor(f"bank{i}", [P, 512], FP32)) for i in range(8)]
        up_ps, y_ps, t_ps = bank[0:4], bank[4:6], bank[6:8]
        rows16 = rows[:, :, :, :, 0:P].bitcast(FP16)
        xt16 = xt[:, :, :, 0:P].bitcast(FP16)
        logit_ps, rank_ps = bank[2], bank[3]
        t16 = [t[:, :].bitcast(FP16) for t in t_ps]

        s_xin = [sem(f"s_xin{g}") for g in range(BATCH)]
        s_small = sem("s_small")
        s_w = [sem(f"s_w{i}") for i in range(2)]
        s_pool = sem("s_pool")
        s_b2 = sem("s_b2")
        s_const = sem("s_const")
        s_wh = sem("s_wh")
        s_wl = sem("s_wl")
        s_b1u = sem("s_b1u")
        s_rstd = sem("s_rstd")
        s_xn = sem("s_xn")
        s_tr = sem("s_tr")
        s_xnt = sem("s_xnt")
        s_hi = sem("s_hi")
        s_low = sem("s_low")
        s_ypair = sem("s_ypair")
        s_logit = sem("s_logit")
        s_lg = sem("s_lg")
        s_dif = sem("s_dif")
        s_edif = sem("s_edif")
        s_oh = sem("s_oh")
        s_rank = sem("s_rank")
        s_slot = sem("s_slot")
        s_sent = sem("s_sent")
        s_cnt = sem("s_cnt")
        s_tab = sem("s_tab")
        s_pad = sem("s_pad")
        s_chain = sem("s_chain")
        s_xt = [sem(f"s_xt{i}") for i in range(STEP)]
        s_t = sem("s_t")
        s_xtt = sem("s_xtt")
        s_dest = sem("s_dest")
        s_bias = [sem(f"s_bias{i}") for i in range(STEP)]
        s_up = [sem(f"s_up{j}") for j in range(HB)]
        s_gate = [sem(f"s_gate{j}") for j in range(HB)]
        s_act = [sem(f"s_act{j}") for j in range(HB)]
        s_acth = [sem(f"s_acth{i}") for i in range(2)]
        s_actl = [sem(f"s_actl{i}") for i in range(2)]
        s_down = sem("s_down")
        s_yout = sem("s_yout")
        s_ygo = sem("s_ygo")
        s_xgo = sem("s_xgo")
        s_ysent = [sem(f"s_ysent{i}") for i in range(STEP)]
        s_yin = [sem(f"s_yin{i}") for i in range(2)]
        s_x1 = sem("s_x1")
        s_bsc = sem("s_bsc")
        s_btr = sem("s_btr")
        s_bt = sem("s_bt")
        s_bu = sem("s_bu")
        s_bud = sem("s_bud")
        s_prod = sem("s_prod")
        s_cx = sem("s_cx")
        s_x2 = sem("s_x2")
        s_x3 = sem("s_x3")
        s_out = sem("s_out")

        order = [("ffn", 0, g) for g in range(BATCH)]
        order += [("lru", 0, 0), ("lru", 0, 1), ("lru", 0, 2), ("ffn", 1, 0), ("lru", 0, 3)]
        order += [("ffn", 1, g) for g in range(1, BATCH)]
        number = {inst: n for n, inst in enumerate(order)}

        def xnt_of(n):
            kind, f, g = order[n]
            return g % 2 if kind == "lru" else 2

        def sent_before(f, tile):
            count = lambda n: (n - tile % STEP + STEP - 1) // STEP
            return f * count(NTILE) + count(tile)

        def wait(eng, semaphore, value):
            if not (isinstance(value, int) and value <= 0):
                eng.wait_ge(semaphore, value)

        def expert_tiles(eng, f, tile):
            def peeled(t):
                tile(t, t, lambda u: f * NTILE + t + u, lambda u, each: each * sent_before(f, t + u))

            for t in range(PEEL):
                peeled(t)
            with eng.Fori(H0, H1) as h:
                made = {}

                def value(step, const):
                    if (step, const) not in made:
                        made[step, const] = eng.snap(h * step + const)
                    return made[step, const]

                for t in range(PEEL, PEEL + STEP):
                    tile(t, value(STEP, t - STEP), lambda u: value(STEP, f * NTILE + t + u - STEP),
                         lambda u, each: value(each, each * (sent_before(f, t + u) - 1)))
            for t in range(REST, NTILE):
                peeled(t)

        block = ctx.enter_context(nc.Block())

        @block.sync
        def _(sp):
            small = [(rwt[:, :], router_t), (rbb[:, :], router_b.partition_broadcast(P)),
                     (b1g[:, :, :], b1_t), (b2b[:, 0, :], b2.partition_broadcast(2)),
                     (bst[:, 0, :], b_re), (bst[:, 1, :], b_im), (ct_re[:, :], c_re_t), (ct_im[:, :], c_im_t),
                     (vec[:, 0:1], nu_log), (vec[:, 1:2], theta_log), (vec[:, 3:4], d_vec), (vec[:, 2:3], gamma_log)]
            for g in range(BATCH):
                for c in range(2):
                    ts = slice(c * GT // 2, (c + 1) * GT // 2)
                    sp.dma_start(xres[:, g, ts, :], x[g].rearrange("(t p) d -> p t d", p=P)[:, ts, :])\
                        .then_inc(s_xin[g], 16)
                if g == 0:
                    for dst, src in small:
                        sp.dma_start(dst, src).then_inc(s_small, 16)
            for e in range(NE):
                if e >= 2:
                    sp.wait_ge(s_wl, 2 * (e - 1))
                sp.dma_start(wst[:, e % 2, 0:2 * HID], w1_t[:, e, :]).then_inc(s_w[e % 2], 16)
                sp.dma_start(wst[:, e % 2, 2 * HID:], w2_t[:, e, :]).then_inc(s_w[e % 2], 16)

            for f in range(2):
                sp.wait_ge(s_tab, f + 1)
                for e in range(NE):
                    row0 = sp.value_load(pad_i[0:1, f, e:e + 1], min_val=0, max_val=NE * REG - SLOT)
                    sp.dma_start(rows_dram[f][bass.ds(row0, SLOT), :].rearrange("(p r) w -> p r w", r=2),
                                 padrow[:, :, :]).then_inc(s_pad, 16)
                sp.dma_start(rows_dram[f][NE * REG:NE * REG + SLOT, :].rearrange("(p r) w -> p r w", r=2),
                             padrow[:, :, :]).then_inc(s_pad, 16)
                sp.wait_ge(s_sent, 16 * TOPK * BATCH * GT * (f + 1))
                sp.wait_ge(s_pad, 16 * (NE + 1) * (f + 1))

                def load(t, s, n, dma):
                    row0 = sp.value_load(toff_i[0:1, f, bass.ds(s, 1)], min_val=0, max_val=NE * REG)
                    wait(sp, s_t, n(1 - STEP))
                    wait(sp, s_dest, n(1 - STEP))
                    sp.dma_start(xt[:, t % STEP, :, :],
                                 rows_dram[f][bass.ds(row0, SLOT), :].rearrange("(p r) w -> p r w", r=2))\
                        .then_inc(s_xt[t % STEP], 16)
                    expert = sp.value_load(tex_i[0:1, f, bass.ds(s, 1)], min_val=0, max_val=NE - 1)
                    wait(sp, s_act[HB - 1], n(1 - STEP))
                    sp.dma_start(bias[:, t % STEP, :].unsqueeze(1), b1g[:, bass.ds(expert, 1), :])\
                        .then_inc(s_bias[t % STEP], 16)

                sp.wait_ge(s_b1u, 1)
                expert_tiles(sp, f, load)
                for t in range(NTILE - STEP, NTILE):
                    sp.wait_ge(s_ysent[t % STEP], 32 * (sent_before(f, t) + 1))
                for g in range(BATCH):
                    n = f * BATCH + g
                    if n >= 2:
                        sp.wait_ge(s_x1, n - 1)
                    for k in range(TOPK):
                        sp.dma_start(yin[:, n % 2, k, :, :],
                                     y_dram[f].rearrange("(k b t p) d -> k b p t d", k=TOPK, b=BATCH, p=P)[k, g])\
                            .then_inc(s_yin[n % 2], 16)
            for g in range(BATCH):
                sp.wait_ge(s_x1, BATCH + g + 1)
                sp.dma_start(out[g].rearrange("(t p) d -> p t d", p=P), xres[:, g, :, :]).then_inc(s_out, 16)
            sp.wait_ge(s_out, 16 * BATCH)

        @block.gpsimd
        def _(pool):
            pool.memset(ident[:, :], 0.0).then_inc(s_pool, 1)
            pool.memset(before[:, :], 1.0).then_inc(s_pool, 1)
            pool.iota(rev_i[:, 0:NE], pattern=[[-1, NE]], base=NE, channel_multiplier=0).then_inc(s_pool, 1)
            pool.iota(rev_i[:, NE:2 * NE], pattern=[[REG, NE]], base=0, channel_multiplier=0).then_inc(s_pool, 1)
            pool.iota(rev_i[:, 2 * NE:], pattern=[[1, NTILE]], base=0, channel_multiplier=0).then_inc(s_pool, 1)
            pool.iota(dest_i[:, :, :, :], pattern=[[TOK, TOPK], [SEQ, BATCH], [P, GT]], base=0,
                      channel_multiplier=1).then_inc(s_pool, 1)
            pool.wait_ge(s_pool, 2)
            pool.affine_select(out=ident[:, :], in_=ident[:, :], compare_op=ALU.not_equal, fill=1.0, base=0,
                               pattern=[[-1, P]], channel_multiplier=1).then_inc(s_pool, 1)
            pool.affine_select(out=before[:, :], in_=before[:, :], compare_op=ALU.is_gt, fill=0.0, base=0,
                               pattern=[[1, P]], channel_multiplier=-1).then_inc(s_pool, 1)
            pool.memset(ones16[:, :], 1.0).then_inc(s_pool, 1)

            for m in range(TURNS):
                ins = pool.memset(double[:, m:m + 1], float(1 << m))
            ins.then_inc(s_pool, 1)

            def send_rows(f, g):
                pool.wait_ge(s_slot, f * BATCH + g + 1)
                for k in range(TOPK):
                    for t in range(GT):
                        pool.indirect_dma_start(
                            out=rows_dram[f], out_offset=bass.IndirectOffsetOnAxis(ap=slot_i[:, k, f, g, t:t + 1], axis=0),
                            in_=rows[:, k, g, t, :], in_offset=None).then_inc(s_sent, 16)

            last_row = pool.to_reg(TOPK * TOK - 1)

            def take_meta(t, n, dma):
                pool.wait_ge(s_xt[t % STEP], dma(STEP, 16))
                wait(pool, s_ysent[t % STEP], dma(0, 32))
                pool.sem_inc(s_xgo, 1)
                pool.tensor_copy(dest[:, t % STEP, :], xt[:, t % STEP, :, P])
                pool.tensor_copy(weight[:, t % STEP, :], xt[:, t % STEP, :, P + 1]).then_inc(s_dest, 1)

            def send_y(f, t, n):
                pool.wait_ge(s_yout, n(1))
                pool.sem_inc(s_ygo, 1)
                for r in range(2):
                    pool.indirect_dma_start(
                        out=y_dram[f],
                        out_offset=bass.IndirectOffsetOnAxis(ap=dest[:, t % STEP, r:r + 1], axis=0),
                        in_=yout[:, t % STEP, r, :], in_offset=None, bounds_check=last_row,
                        oob_is_err=False).then_inc(s_ysent[t % STEP], 16)

            def pair_outputs(f, g):
                n = f * BATCH + g
                pool.wait_ge(s_yin[n % 2], 16 * TOPK * (n // 2 + 1))
                pool.tensor_tensor(yin[:, n % 2, 0, :, :], yin[:, n % 2, 0, :, :], yin[:, n % 2, 1, :, :],
                                   ALU.add).then_inc(s_ypair, 1)

            for f in range(2):
                for g in range(BATCH):
                    send_rows(f, g)
                take_meta(0, lambda u: f * NTILE + u, lambda u, each: each * sent_before(f, u))

                def tile(t, s, n, dma):
                    if t + 1 < NTILE:
                        take_meta(t + 1, lambda u: n(u + 1), lambda u, each: dma(u + 1, each))
                    send_y(f, t, n)

                expert_tiles(pool, f, tile)
                for g in range(BATCH):
                    pair_outputs(f, g)

        @block.scalar
        def _(act_e):
            def normalise(n):
                kind, f, g = order[n]
                act_e.wait_ge(s_rstd, n + 1)
                if n >= 2:
                    act_e.wait_ge(s_tr, 2 * (n - 1))
                    kind2, f2, g2 = order[n - 2]
                    if kind2 == "ffn":
                        act_e.wait_ge(s_low, f2 * BATCH + g2 + 1)
                for t in range(GT):
                    ins = nc.scalar.activation(xn[:, n % 2, t, :], xres[:, g, t, :], ACT.Identity,
                                               scale=rstd[:, n % 2, t:t + 1], bias=shift[:, n % 2, t:t + 1])
                ins.then_inc(s_xn, 1)

            def transposed(n):
                kind, f, g = order[n]
                if kind == "ffn" and f * BATCH + g > 0:
                    act_e.wait_ge(s_logit, f * BATCH + g)
                if kind == "lru" and g >= 2:
                    act_e.wait_ge(s_cx, 2 * (g - 1))
                for c in range(2):
                    act_e.wait_ge(s_tr, 2 * n + c + 1)
                    nc.scalar.copy(xnt[:, xnt_of(n), c * HALF:(c + 1) * HALF], t_ps[c][:, :]).then_inc(s_xnt, 1)

            def high_part(f, g):
                n = number["ffn", f, g]
                act_e.wait_ge(s_xn, n + 1)
                if f > 0:
                    act_e.wait_ge(s_sent, 16 * TOPK * BATCH * GT)
                nc.scalar.copy(rows16[:, 0, g, :, 0:P], xn[:, n % 2, :, :]).then_inc(s_hi, 1)

            def exp_dif(f, g):
                q = f * BATCH + g
                act_e.wait_ge(s_dif, q + 1)
                nc.scalar.activation(edif[:, q % 2, :], dif[:, q % 2, :], ACT.Exp).then_inc(s_edif, 1)

            def weight_high(e):
                act_e.wait_ge(s_w[e % 2], 32 * (e // 2 + 1))
                nc.scalar.mul(w1h[:, e * 2 * HID:(e + 1) * 2 * HID], wst[:, e % 2, 0:2 * HID], WS).then_inc(s_wh, 1)
                nc.scalar.mul(w2h[:, e * HB * P:(e + 1) * HB * P], wst[:, e % 2, 2 * HID:], WS).then_inc(s_wh, 1)

            normalise(0)
            transposed(0)
            high_part(0, 0)
            for g in range(BATCH):
                if g + 1 < BATCH:
                    normalise(g + 1)
                    transposed(g + 1)
                    high_part(0, g + 1)
                exp_dif(0, g)
                for e in (2 * g, 2 * g + 1):
                    weight_high(e)
            nc.scalar.mul(b2b[:, 1, :], b2b[:, 0, :], WS * WS).then_inc(s_b2, 1)
            act_e.wait_ge(s_b2, 1)
            nc.scalar.copy(b2h[:, 0, 0:NE * P], b2b[:, 1, :]).then_inc(s_b2, 1)
            act_e.wait_ge(s_b2, 2)
            nc.scalar.mul(b2h[:, 1, 0:NE * P], b2h[:, 0, 0:NE * P], ident[0:2, 0:1]).then_inc(s_b2, 1)
            act_e.wait_ge(s_btr, 1)
            nc.scalar.copy(bt[:, :, :], t_ps[0][:, 0:2 * P].rearrange("p (a d) -> p a d", a=2)).then_inc(s_bt, 1)

            def gates(t, j, n):
                act_e.wait_ge(s_up[j], n(1))
                nc.scalar.activation(gate[:, j, :], up_ps[j][:, 0:SLOT], ACT.Silu, scale=1.0 / WS,
                                     bias=bias[:, t % STEP, j:j + 1]).then_inc(s_gate[j], 1)

            def act_high(t, half, n):
                act_e.wait_ge(s_act[2 * half + 1], n(1))
                if half == 0:
                    wait(act_e, s_down, n(1 - BUFS))
                nc.scalar.copy(acth[:, t % BUFS, 2 * half:2 * half + 2, :],
                               act[:, 2 * half:2 * half + 2, :]).then_inc(s_acth[half], 1)

            def weighted(t, n, dma):
                act_e.wait_ge(s_dest, n(1))
                wait(act_e, s_ysent[t % STEP], dma(0, 32))
                act_e.wait_ge(s_down, n(1))
                for r in range(2):
                    ins = nc.scalar.mul(yout[:, t % STEP, r, :], y_ps[t % BUFS][:, r * P:(r + 1) * P],
                                        weight[:, t % STEP, r:r + 1])
                ins.then_inc(s_yout, 1)

            def tile(t, s, n, dma):
                act_e.wait_ge(s_bias[t % STEP], dma(STEP, 16))
                gates(t, 0, n)
                gates(t, 1, n)
                gates(t, 2, n)
                act_high(t, 0, n)
                gates(t, 3, n)
                act_high(t, 1, n)
                if t >= 1:
                    weighted(t - 1, lambda u: n(u - 1), lambda u, each: dma(u - 1, each))

            for f in range(2):
                if f > 0:
                    for n in (number["lru", 0, 0], number["lru", 0, 1]):
                        normalise(n)
                        transposed(n)
                    for g in range(BATCH):
                        if g == 0:
                            normalise(number["lru", 0, 2])
                            transposed(number["lru", 0, 2])
                        if g == 1:
                            normalise(number["lru", 0, 3])
                            transposed(number["lru", 0, 3])
                        normalise(number["ffn", 1, g])
                        transposed(number["ffn", 1, g])
                        high_part(1, g)
                        exp_dif(1, g)
                act_e.wait_ge(s_tab, f + 1)

                expert_tiles(act_e, f, tile)
                t = NTILE - 1
                weighted(t, lambda u: f * NTILE + t + u, lambda u, each: each * sent_before(f, t + u))

        @block.vector
        def _(dve):
            count = [0]

            def link(ins):
                count[0] += 1
                ins.then_inc(s_chain, 1)
                dve.wait_ge(s_chain, count[0])

            V = nc.vector

            def over_e(a):
                return a.unsqueeze(2).to_broadcast([P, GT, NE])

            def over_t(a):
                return a.unsqueeze(1).to_broadcast([P, GT, NE])

            V.memset(ones8[:, :], 1.0)
            V.memset(seen[:, :, 0, :], 0.0)
            link(V.memset(padrow[:, :, :], 0.0))
            link(V.memset(padrow[:, :, P:P + 1], float(OUTSIDE)))
            dve.wait_ge(s_pool, 9)
            V.tensor_copy(ident16[:, :], ident[:, :]).then_inc(s_const, 1)
            link(V.tensor_copy(rev_f[:, :], rev_i[:, :]))
            for k in range(TOPK):
                for g in range(BATCH):
                    ins = V.tensor_copy(rows[:, k, g, :, P:P + 1],
                                        dest_i[:, k, g, :].unsqueeze(2))
            link(ins)

            def statistics(n):
                kind, f, g = order[n]
                for t in range(GT):
                    ins = V.bn_stats(bn[:, t, :], xres[:, g, t, :])
                link(ins)
                if n >= 2:
                    dve.wait_ge(s_xn, n - 1)
                for t in range(GT):
                    ins = V.bn_aggr(mv[:, n % 2, t, :], bn[:, t, :])
                link(ins)
                r, r_i = rstd[:, n % 2, :], rstd[:, n % 2, :].bitcast(I32)
                v, square, minus_half_v = [newton[:, i, :] for i in range(3)]
                link(V.tensor_scalar(v, mv[:, n % 2, :, 1], EPS, None, ALU.add))
                V.tensor_scalar(minus_half_v, v, -0.5, None, ALU.mult)
                link(V.tensor_scalar(guess_i[:, :], v.bitcast(I32), 1, None, ALU.logical_shift_right))
                link(V.tensor_scalar(r_i, guess_i[:, :], -1.0, float(0x5f3759df), ALU.mult, ALU.add))
                for _ in range(3):
                    link(V.tensor_tensor(square, r, r, ALU.mult))
                    link(V.tensor_tensor(square, square, minus_half_v, ALU.mult))
                    link(V.scalar_tensor_tensor(r, square, 1.5, r, ALU.add, ALU.mult))
                V.scalar_tensor_tensor(shift[:, n % 2, :], mv[:, n % 2, :, 0], -1.0, rstd[:, n % 2, :],
                                       ALU.mult, ALU.mult).then_inc(s_rstd, 1)

            def row_parts(f, g):
                n = number["ffn", f, g]
                dve.wait_ge(s_hi, f * BATCH + g + 1)
                V.tensor_tensor(rows16[:, 0, g, :, P:2 * P], xn[:, n % 2, :, :], rows16[:, 0, g, :, 0:P],
                                ALU.subtract).then_inc(s_low, 1)
                dve.wait_ge(s_low, f * BATCH + g + 1)
                link(V.tensor_copy(rows16[:, 1, g, :, :], rows16[:, 0, g, :, :]))

            def pick(o, m):
                link(V.tensor_reduce(m[:, :], lg[:, :, :], AX, ALU.max))
                link(V.tensor_tensor(tmp8[:, :, :], lg[:, :, :], over_e(m[:, :]), ALU.is_ge))
                link(V.tensor_tensor(tmp8[:, :, :], tmp8[:, :, :], over_t(rev_f[:, 0:NE]), ALU.mult))
                link(V.tensor_reduce(rr[:, :], tmp8[:, :, :], AX, ALU.max))
                link(V.tensor_tensor(o[:, :, :], tmp8[:, :, :], over_e(rr[:, :]), ALU.is_equal))

            def choose(f, g):
                q = f * BATCH + g
                dve.wait_ge(s_logit, q + 1)
                link(V.tensor_tensor(lg[:, :, :], logit_ps[:, 0:GT * NE].rearrange("p (t e) -> p t e", e=NE),
                                     over_t(rbb[:, :]), ALU.add))
                pick(oh1, m1)
                link(V.scalar_tensor_tensor(lg[:, :, :].rearrange("p t e -> p (t e)"),
                                            oh1[:, :, :].rearrange("p t e -> p (t e)"), -BIG,
                                            lg[:, :, :].rearrange("p t e -> p (t e)"), ALU.mult, ALU.add))
                pick(oh2, m2)
                V.tensor_tensor(dif[:, q % 2, :], m2[:, :], m1[:, :], ALU.subtract).then_inc(s_dif, 1)
                V.tensor_tensor(oh[:, q % 2, :, :], oh1[:, :, :], oh2[:, :, :], ALU.add).then_inc(s_oh, 1)
                dve.wait_ge(s_oh, q + 1)
                link(V.tensor_reduce(seen1[:, :], oh[:, q % 2, :, :].rearrange("p t e -> p e t"), AX, ALU.add))
                V.tensor_tensor(seen[:, f, g + 1, :], seen[:, f, g, :], seen1[:, :], ALU.add).then_inc(s_lg, 1)

            def weights_and_slots(f, g):
                q = f * BATCH + g
                dve.wait_ge(s_edif, q + 1)
                link(V.tensor_scalar(den[:, :], edif[:, q % 2, :], 1.0, 2.0 * WS * WS, ALU.add, ALU.mult))
                link(V.reciprocal(wk[:, 0, :], den[:, :]))
                link(V.tensor_tensor(wk[:, 1, :], wk[:, 0, :], edif[:, q % 2, :], ALU.mult))
                for k in range(TOPK):
                    link(V.tensor_copy(rows[:, k, g, :, P + 1:P + 2], wk[:, k, :].unsqueeze(2)))
                dve.wait_ge(s_rank, q + 1)
                link(V.tensor_tensor(slotf[:, :, :], rank_ps[:, 0:GT * NE].rearrange("p (t e) -> p t e", e=NE),
                                     over_t(rev_f[:, NE:2 * NE]), ALU.add))
                for k, o in enumerate((oh1, oh2)):
                    link(V.tensor_tensor(tmp8[:, :, :], slotf[:, :, :], o[:, :, :], ALU.mult))
                    link(V.tensor_reduce(slot1[:, :], tmp8[:, :, :], AX, ALU.add))
                    ins = V.tensor_copy(slot_i[:, k, f, g, :], slot1[:, :])
                    if k == 0:
                        link(ins)
                ins.then_inc(s_slot, 1)

            def tile_table(f):
                dve.wait_ge(s_cnt, f + 1)
                link(V.tensor_copy(cnt[:, :], rank_ps[:, 128:128 + NE]))
                link(V.tensor_scalar(cnt_i[:, :], cnt[:, :], float(SLOT - 1), None, ALU.add))
                link(V.tensor_scalar(cnt_i[:, :], cnt_i[:, :], SLOT.bit_length() - 1, None, ALU.logical_shift_right))
                link(V.tensor_copy(ntile[:, :], cnt_i[:, :]))
                link(V.tensor_tensor_scan(upto[:, :], ones8[:, :], ntile[:, :], 0.0, ALU.mult, ALU.add))
                link(V.tensor_tensor(pad_i[:, f, :], cnt[:, :], rev_f[:, NE:2 * NE], ALU.add))
                tiles = rev_f[:, 2 * NE:]

                def grid(a):
                    return a.unsqueeze(1).to_broadcast([P, NTILE, NE])

                link(V.tensor_tensor(ge_hi[:, :, :], tiles.unsqueeze(2).to_broadcast([P, NTILE, NE]),
                                     grid(upto[:, :]), ALU.is_ge))
                link(V.tensor_reduce(tex[:, :], ge_hi[:, :, :], AX, ALU.add))
                link(V.tensor_tensor(ntile[:, :], upto[:, :], ntile[:, :], ALU.subtract))
                link(V.tensor_tensor(ge_lo[:, :, :], tiles.unsqueeze(2).to_broadcast([P, NTILE, NE]),
                                     grid(ntile[:, :]), ALU.is_ge))
                link(V.tensor_tensor(ge_lo[:, :, :], ge_lo[:, :, :], ge_hi[:, :, :], ALU.subtract))
                link(V.scalar_tensor_tensor(base8[:, :], ntile[:, :], -float(SLOT), rev_f[:, NE:2 * NE],
                                            ALU.mult, ALU.add))
                link(V.tensor_tensor(ge_lo[:, :, :], ge_lo[:, :, :], grid(base8[:, :]), ALU.mult))
                link(V.tensor_reduce(toff[:, :], ge_lo[:, :, :], AX, ALU.add))
                link(V.scalar_tensor_tensor(toff[:, :], tiles, float(SLOT), toff[:, :], ALU.mult, ALU.add))
                unused = ge_hi[:, :, NE - 1]
                link(V.scalar_tensor_tensor(ge_lo[:, :, 0], tiles, -float(SLOT), unused, ALU.mult, ALU.mult))
                link(V.scalar_tensor_tensor(ge_lo[:, :, 0], unused, float(NE * REG), ge_lo[:, :, 0],
                                            ALU.mult, ALU.add))
                link(V.tensor_tensor(toff_i[:, f, :], toff[:, :], ge_lo[:, :, 0], ALU.add))
                V.tensor_scalar(tex_i[:, f, :], tex[:, :], float(NE - 1), None, ALU.min).then_inc(s_tab, 1)
                dve.wait_ge(s_tab, f + 1)

            def weight_low(e):
                for i, (hi, lo, a, b) in enumerate(((w1h, w1l, 0, 2 * HID), (w2h, w2l, 2 * HID, 2 * HID + HB * P))):
                    w = b - a
                    dve.wait_ge(s_wh, 2 * e + i + 1)
                    V.scalar_tensor_tensor(lo[:, e * w:(e + 1) * w], wst[:, e % 2, a:b], WS, hi[:, e * w:(e + 1) * w],
                                           ALU.mult, ALU.subtract).then_inc(s_wl, 1)

            def horner(acc, z, coefficients):
                link(V.tensor_scalar(acc, z, coefficients[0], None, ALU.mult))
                for c in coefficients[1:-1]:
                    link(V.scalar_tensor_tensor(acc, acc, c, z, ALU.add, ALU.mult))
                link(V.tensor_scalar(acc, acc, coefficients[-1], None, ALU.add))

            def exponential(dst, src, w):
                t, k, acc = [ex[:, i, 0:w] for i in range(3)]
                k_i, two_k = [ex_i[:, i, 0:w] for i in range(2)]
                link(V.tensor_scalar(t, src, -87.0, 88.0, ALU.max, ALU.min))
                link(V.tensor_scalar(k_i, t, LOG2_E, None, ALU.mult))
                link(V.tensor_copy(k, k_i))
                link(V.scalar_tensor_tensor(t, k, -LN2_HIGH, t, ALU.mult, ALU.add))
                link(V.scalar_tensor_tensor(t, k, -LN2_LOW, t, ALU.mult, ALU.add))
                link(V.tensor_scalar(two_k, k, 127.0, float(1 << 23), ALU.add, ALU.mult))
                factorial, coefficients = 1.0, [1.0]
                for i in range(1, 10):
                    factorial *= i
                    coefficients.insert(0, 1.0 / factorial)
                horner(acc, t, coefficients)
                link(V.tensor_tensor(dst, acc, two_k.bitcast(FP32), ALU.mult))

            def lru_constants():
                exponential(lam[:, 0:3], vec[:, 0:3], 3)
                link(V.tensor_scalar(lam[:, 0:1], lam[:, 0:1], -1.0, None, ALU.mult))
                exponential(lam[:, 3:4], lam[:, 0:1], 1)
                for i in range(2):
                    ins = V.tensor_scalar(bst[:, i, :], bst[:, i, :], lam[:, 2:3], None, ALU.mult)
                ins.then_inc(s_bsc, 1)
                V.tensor_scalar(diag_d[:, :], ident[:, :], vec[:, 3:4], None, ALU.mult)
                V.tensor_scalar(nct_re[:, :], ct_re[:, :], -1.0, None, ALU.mult)
                V.tensor_scalar(nct_im[:, :], ct_im[:, :], -1.0, None, ALU.mult)
                angle, turns, half, square, sine, cosine, c_all, s_all = [trig[:, i, :] for i in range(8)]
                dve.wait_ge(s_pool, 10)
                link(V.tensor_scalar(angle, double[:, :], lam[:, 1:2], None, ALU.mult))
                link(V.tensor_scalar(turns_i[:, :], angle, 1.0 / TWO_PI, None, ALU.mult))
                link(V.tensor_copy(turns, turns_i[:, :]))
                for part in TWO_PI_PARTS:
                    link(V.scalar_tensor_tensor(angle, turns, -part, angle, ALU.mult, ALU.add))
                link(V.tensor_scalar(half, angle, 0.5, None, ALU.mult))
                link(V.tensor_tensor(square, half, half, ALU.mult))
                by_power, factorial = ([1.0], [1.0]), 1.0
                for i in range(2, 18):
                    factorial *= i
                    by_power[(i + 1) % 2].insert(0, (-1.0 if (i // 2) % 2 else 1.0) / factorial)
                of_sine, of_cosine = by_power
                pair = ((sine, of_sine), (cosine, of_cosine))
                for acc, c in pair:
                    ins = V.tensor_scalar(acc, square, c[0], None, ALU.mult)
                link(ins)
                for i in range(1, len(of_sine) - 1):
                    for acc, c in pair:
                        ins = V.scalar_tensor_tensor(acc, acc, c[i], square, ALU.add, ALU.mult)
                    link(ins)
                for acc, c in pair:
                    ins = V.tensor_scalar(acc, acc, c[-1], None, ALU.add)
                link(ins)
                link(V.tensor_tensor(sine, sine, half, ALU.mult))
                V.scalar_tensor_tensor(s_all, sine, 2.0, cosine, ALU.mult, ALU.mult)
                link(V.scalar_tensor_tensor(c_all, sine, -2.0, sine, ALU.mult, ALU.mult))
                link(V.tensor_scalar(c_all, c_all, 1.0, None, ALU.add))
                link(V.tensor_tensor(turns, c_all, c_all, ALU.mult))
                link(V.tensor_tensor(square, s_all, s_all, ALU.mult))
                link(V.tensor_tensor(square, square, turns, ALU.add))
                link(V.tensor_scalar(square, square, -0.5, 1.5, ALU.mult, ALU.add))
                V.tensor_tensor(c_all, c_all, square, ALU.mult)
                V.tensor_tensor(s_all, s_all, square, ALU.mult)
                V.memset(ctab[:, 0:1], 1.0)
                link(V.memset(stab[:, 0:1], 0.0))
                for m in range(TURNS):
                    n = 1 << m
                    c_n, s_n = c_all[:, m:m + 1], s_all[:, m:m + 1]
                    V.tensor_scalar(prod[:, 0, 0:n], stab[:, 0:n], s_n, None, ALU.mult)
                    link(V.tensor_scalar(prod[:, 1, 0:n], ctab[:, 0:n], s_n, None, ALU.mult))
                    V.scalar_tensor_tensor(ctab[:, n:2 * n], ctab[:, 0:n], c_n, prod[:, 0, 0:n],
                                           ALU.mult, ALU.subtract)
                    link(V.scalar_tensor_tensor(stab[:, n:2 * n], stab[:, 0:n], c_n, prod[:, 1, 0:n],
                                                ALU.mult, ALU.add))

            def add_outputs(f, g):
                n = f * BATCH + g
                dve.wait_ge(s_ypair, n + 1)
                V.tensor_tensor(xres[:, g, :, :], xres[:, g, :, :], yin[:, n % 2, 0, :, :], ALU.add).then_inc(s_x1, 1)
                dve.wait_ge(s_x1, n + 1)

            def recurrence(g):
                for c in range(2):
                    cols = slice(c * HALF, (c + 1) * HALF)
                    dve.wait_ge(s_bu, 2 * g + c + 1)
                    re, im = up_ps[0][:, :], up_ps[1][:, :]
                    V.tensor_tensor(rot[0][:, :], ctab[:, cols], re, ALU.mult)
                    V.tensor_tensor(rot[1][:, :], stab[:, cols], im, ALU.mult)
                    V.tensor_tensor(rot[2][:, :], ctab[:, cols], im, ALU.mult)
                    ins = V.tensor_tensor(rot[3][:, :], stab[:, cols], re, ALU.mult)
                    ins.then_inc(s_bud, 1)
                    dve.wait_ge(s_bud, 2 * g + c + 1)
                    V.tensor_tensor(rot[0][:, :], rot[0][:, :], rot[1][:, :], ALU.add)
                    link(V.tensor_tensor(rot[2][:, :], rot[2][:, :], rot[3][:, :], ALU.subtract))
                    decay = lam[:, 3:4].to_broadcast([P, HALF])
                    for y, v in ((yre, rot[0]), (yim, rot[2])):
                        start = 0.0 if c == 0 else y[:, HALF - 1:HALF]
                        ins = V.tensor_tensor_scan(y[:, cols], decay, v[:, :], start, ALU.mult, ALU.add)
                    link(ins)
                    if g > 0:
                        dve.wait_ge(s_cx, 2 * (g - 1) + c + 1)
                    for i, (y, tab) in enumerate(((yre, ctab), (yim, stab), (yre, stab), (yim, ctab))):
                        ins = V.tensor_tensor(prod[:, i, cols], y[:, cols], tab[:, cols], ALU.mult)
                    ins.then_inc(s_prod, 1)

            def add_recurrence(g):
                for c in range(2):
                    dve.wait_ge(s_cx, 2 * g + c + 1)
                    sl = xres[:, g, 4 * c:4 * c + 4, :].rearrange("p t d -> p (t d)")
                    ins = V.tensor_tensor(sl, sl, y_ps[c][:, :], ALU.add)
                ins.then_inc(s_x2, 1)
                dve.wait_ge(s_x2, g + 1)

            def first_statistics(g):
                dve.wait_ge(s_xin[g], 32)
                statistics(g)

            first_statistics(0)
            dve.wait_ge(s_small, 16 * 12)
            V.tensor_scalar(b1g[:, :, HB:2 * HB], b1g[:, :, HB:2 * HB], WS, None, ALU.mult).then_inc(s_b1u, 1)
            for g in range(BATCH):
                if g + 1 < BATCH:
                    first_statistics(g + 1)
                row_parts(0, g)
                choose(0, g)
                if g > 0:
                    weight_low(2 * g - 2)
                weights_and_slots(0, g)
                if g > 0:
                    weight_low(2 * g - 1)
            tile_table(0)
            for e in (NE - 2, NE - 1):
                weight_low(e)
            dve.wait_ge(s_b2, 3)
            link(V.tensor_tensor(b2b[:, 0, :], b2b[:, 1, :], b2h[:, 0, 0:NE * P], ALU.subtract))
            V.scalar_tensor_tensor(b2p[:, :], b2b[:, 0, :], ident[0:2, 1:2], b2h[:, 1, 0:NE * P],
                                   ALU.mult, ALU.add).then_inc(s_b2, 1)
            lru_constants()

            def take_tile(t, n):
                dve.wait_ge(s_t, n(1))
                V.tensor_copy(xt_t[:, t % BUFS, :, :].rearrange("p a s -> p (a s)"),
                              t16[t % BUFS][:, 0:2 * SLOT]).then_inc(s_xtt, 1)

            def activate(t, j, n):
                wait(dve, s_actl[j // 2], n(0))
                dve.wait_ge(s_gate[j], n(1))
                V.scalar_tensor_tensor(act[:, j, :], up_ps[j][:, SLOT:], bias[:, t % STEP, HB + j:HB + j + 1],
                                       gate[:, j, :], ALU.add, ALU.mult).then_inc(s_act[j], 1)

            def act_low(t, half, n):
                dve.wait_ge(s_acth[half], n(1))
                h2 = slice(2 * half, 2 * half + 2)
                V.tensor_tensor(actl[:, t % BUFS, h2, :], act[:, h2, :], acth[:, t % BUFS, h2, :],
                                ALU.subtract).then_inc(s_actl[half], 1)

            def tile(t, s, n, dma):
                if t < NTILE - 1:
                    take_tile(t + 1, lambda u: n(u + 1))
                for j in range(3):
                    activate(t, j, n)
                act_low(t, 0, n)
                activate(t, 3, n)
                act_low(t, 1, n)

            for f in range(2):
                if f > 0:
                    for g in range(2):
                        add_outputs(0, g)
                        statistics(number["lru", 0, g])
                    recurrence(0)
                    add_outputs(0, 2)
                    statistics(number["lru", 0, 2])
                    for g in range(BATCH):
                        add_recurrence(g)
                        statistics(number["ffn", 1, g])
                        if g + 1 < BATCH:
                            recurrence(g + 1)
                        row_parts(1, g)
                        choose(1, g)
                        if g == 0:
                            add_outputs(0, 3)
                            statistics(number["lru", 0, 3])
                        weights_and_slots(1, g)
                    tile_table(1)

                take_tile(0, lambda u: f * NTILE + u)
                expert_tiles(dve, f, tile)
            for g in range(BATCH):
                add_outputs(1, g)

        @block.tensor
        def _(pe):
            T = nc.tensor

            def transpose_rows(n):
                pe.wait_ge(s_xn, n + 1)
                for c in range(2):
                    if n >= 1:
                        pe.wait_ge(s_xnt, 2 * (n - 1) + c + 1)
                    for j in range(4):
                        ins = T.transpose(t_ps[c][:, j * P:(j + 1) * P], xn[:, n % 2, 4 * c + j, :], ident[:, :])
                    ins.then_inc(s_tr, 1)

            def logits(f, g):
                n, q = number["ffn", f, g], f * BATCH + g
                pe.wait_ge(s_xnt, 2 * n + 2)
                if q >= 1:
                    pe.wait_ge(s_oh, q)
                for t in range(GT):
                    ins = T.matmul(logit_ps[:, t * NE:(t + 1) * NE], xnt[:, 2, t * P:(t + 1) * P], rwt[:, :],
                                   start=True, stop=True)
                ins.then_inc(s_logit, 1)

            def rank(f, g):
                q = f * BATCH + g
                pe.wait_ge(s_oh, q + 1)
                if q >= 1:
                    pe.wait_ge(s_slot, q)
                ranks = rank_ps[:, 0:GT * NE].rearrange("p (t e) -> p t e", e=NE)
                T.matmul(ranks, before[:, :], oh[:, q % 2, :, :], start=True, stop=False)
                for t in range(GT - 1):
                    m = GT - 1 - t
                    T.matmul(ranks[:, t + 1:, :], ones16[:, :],
                             oh[:, q % 2, t, :].unsqueeze(1).to_broadcast([P, m, NE]), start=False, stop=False)
                T.matmul(ranks, ones16[:, :], seen[:, f, g, :].unsqueeze(1).to_broadcast([P, GT, NE]),
                         start=False, stop=True).then_inc(s_rank, 1)
                if g == BATCH - 1:
                    pe.wait_ge(s_lg, q + 1)
                    pe.wait_ge(s_slot, q + 1)
                    T.matmul(rank_ps[:, 128:128 + NE], ones16[:, :], seen[:, f, BATCH, :],
                             start=True, stop=True).then_inc(s_cnt, 1)

            pe.wait_ge(s_const, 1)
            transpose_rows(0)
            pe.wait_ge(s_small, 16 * 12)
            for g in range(BATCH):
                logits(0, g)
                if g + 1 < BATCH:
                    transpose_rows(g + 1)
                rank(0, g)
            pe.wait_ge(s_bsc, 1)
            pe.wait_ge(s_xnt, 2 * BATCH)
            for i in range(2):
                ins = T.transpose(t_ps[0][:, i * P:(i + 1) * P], bst[:, i, :], ident[:, :])
            ins.then_inc(s_btr, 1)

            def bu(g, c):
                n = number["lru", 0, g]
                pe.wait_ge(s_xnt, 2 * n + c + 1)
                if 2 * g + c > 0:
                    pe.wait_ge(s_bud, 2 * g + c)
                for i in range(2):
                    ins = T.matmul(up_ps[i][:, :], bt[:, i, :], xnt[:, xnt_of(n), c * HALF:(c + 1) * HALF],
                                   start=True, stop=True)
                ins.then_inc(s_bu, 1)

            def cx(g, c):
                pe.wait_ge(s_prod, 2 * g + c + 1)
                if g > 0:
                    pe.wait_ge(s_x2, g)
                for t in range(c * GT // 2, (c + 1) * GT // 2):
                    cols = slice(t * P, (t + 1) * P)
                    o = y_ps[c][:, (t % 4) * P:(t % 4 + 1) * P]
                    terms = [(prod[:, 0, cols], ct_re), (prod[:, 1, cols], nct_re), (prod[:, 2, cols], nct_im),
                             (prod[:, 3, cols], nct_im), (xnt[:, g % 2, cols], diag_d)]
                    for i, (a, m) in enumerate(terms):
                        ins = T.matmul(o, a, m[:, :], start=(i == 0), stop=(i == len(terms) - 1))
                ins.then_inc(s_cx, 1)

            def transpose_tile(t, n, landed):
                pe.wait_ge(s_xt[t % STEP], landed)
                for a in range(2):
                    for r in range(2):
                        ins = T.transpose(t16[t % BUFS][:, (2 * a + r) * P:(2 * a + r + 1) * P],
                                          xt16[:, t % STEP, r, a * P:(a + 1) * P], ident16[:, :])
                ins.then_inc(s_t, 1)

            def expert_of(f, s):
                return nc.values_load(tex_i[0:1, f, bass.ds(s, 1)], engines=[mybir.EngineType.PE], min_val=0,
                                      max_val=NE - 1,
                                      skip_runtime_bounds_check_because="VectorE made the table's experts: "
                                      "0 .. NE, and at most NE - 1")

            def up(e_reg, t, n):
                for j in range(HB):
                    for half in range(2):
                        at = pe.snap(e_reg * (2 * HID) + (half * HID + j * P))
                        if t == 0 and j == 0 and half == 0:
                            pe.wait_ge(s_xtt, n(1))
                        if half == 0:
                            wait(pe, s_act[j], n(0))
                        o = up_ps[j][:, half * SLOT:(half + 1) * SLOT]
                        T.matmul(o, w1h[:, bass.ds(at, P)], xt_t[:, t % BUFS, 0, :], start=True, stop=False)
                        T.matmul(o, w1h[:, bass.ds(at, P)], xt_t[:, t % BUFS, 1, :], start=False, stop=False)
                        ins = T.matmul(o, w1l[:, bass.ds(at, P)], xt_t[:, t % BUFS, 0, :], start=False, stop=True)
                    ins.then_inc(s_up[j], 1)

            def down(e_reg, t, n):
                at = [pe.snap(e_reg * (HB * P) + c * P) for c in range(HB)]
                bias_at = pe.snap(e_reg * P)
                pe.wait_ge(s_actl[1], n(1))
                for r in range(2):
                    o = y_ps[t % BUFS][:, r * P:(r + 1) * P]
                    rs = slice(r * P, (r + 1) * P)
                    T.matmul(o, ones16[0:2, :], b2p[:, bass.ds(bias_at, P)], start=True, stop=False)
                    for c in range(HB):
                        T.matmul(o, acth[:, t % BUFS, c, rs], w2h[:, bass.ds(at[c], P)], start=False, stop=False)
                        T.matmul(o, acth[:, t % BUFS, c, rs], w2l[:, bass.ds(at[c], P)], start=False, stop=False)
                        ins = T.matmul(o, actl[:, t % BUFS, c, rs], w2h[:, bass.ds(at[c], P)], start=False,
                                       stop=(c == HB - 1))
                ins.then_inc(s_down, 1)

            def tile(f, t, s, n, dma, kept):
                if t < NTILE - 1:
                    transpose_tile(t + 1, lambda u: n(u + 1), dma(1 + STEP, 16))
                e_reg = expert_of(f, s)
                up(e_reg, t, n)
                if t >= 1:
                    last = kept["expert"] if t - 1 in kept else expert_of(f, s - 1)
                    down(last, t - 1, lambda u: n(u - 1))
                kept.clear()
                kept[t] = True
                kept["expert"] = e_reg

            for f in range(2):
                b = f * NTILE
                if f > 0:
                    transpose_rows(number["lru", 0, 0])
                    bu(0, 0)
                    transpose_rows(number["lru", 0, 1])
                    bu(0, 1)
                    for g in range(BATCH):
                        cx(g, 0)
                        if g + 1 < BATCH:
                            bu(g + 1, 0)
                        cx(g, 1)
                        if g > 0:
                            rank(1, g - 1)
                        if g < 2:
                            transpose_rows(number["lru", 0, g + 2])
                        transpose_rows(number["ffn", 1, g])
                        if g + 1 < BATCH:
                            bu(g + 1, 1)
                        logits(1, g)
                    rank(1, BATCH - 1)
                else:
                    pe.wait_ge(s_wl, 2 * NE)
                    pe.wait_ge(s_b2, 4)
                    pe.wait_ge(s_bt, 1)
                pe.wait_ge(s_tab, f + 1)

                transpose_tile(0, lambda u: b + u, 16 * (sent_before(f, 0) + 1))
                kept = {}

                def run(t, s, n, dma):
                    if t in (PEEL, REST):
                        kept.clear()
                    tile(f, t, s, n, dma, kept)

                expert_tiles(pe, f, run)
                down(expert_of(f, NTILE - 1), NTILE - 1, lambda u: b + NTILE - 1 + u)


def _laid_out(inputs):
    import numpy as np
    a = {k.replace("L0_", ""): np.asarray(v) for k, v in inputs.items()}
    col = lambda v: v.reshape(P, 1)
    row = lambda v: v.reshape(-1)
    return [
        ("x", a["attn_inputs"]), ("nu_log", col(a["attn_nu_log"])), ("theta_log", col(a["attn_theta_log"])),
        ("b_re", a["attn_B_re"]), ("b_im", a["attn_B_im"]),
        ("c_re_t", a["attn_C_re"].T), ("c_im_t", a["attn_C_im"].T),
        ("d_vec", col(a["attn_D"])), ("gamma_log", col(a["attn_gamma_log"])),
        ("router_t", a["ffn_router_w"].T), ("router_b", row(a["ffn_router_b"])),
        ("w1_t", a["ffn_w1"].transpose(2, 0, 1)),
        ("b1_t", a["ffn_b1"].reshape(NE, 2 * HB, P).transpose(2, 0, 1)),
        ("w2_t", a["ffn_w2"].reshape(NE, P, HB, P).transpose(3, 0, 2, 1).reshape(P, NE, HB * P)),
        ("b2", row(a["ffn_b2"])),
    ]


def kernel(**inputs):
    import numpy as np
    import concourse.bacc as bacc
    from concourse import mybir as mb
    from concourse.bass_utils import run_bass_kernel_spmd

    nc = bacc.Bacc("TRN2", target_bir_lowering=False, num_devices=1)
    arrays, args = {}, []
    for name, a in _laid_out(inputs):
        a = np.ascontiguousarray(a)
        arrays[f"in_{name}"] = a
        args.append(nc.dram_tensor(f"in_{name}", a.shape, mb.dt.from_np(a.dtype), kind="ExternalInput").ap())
    args.append(nc.dram_tensor("out_0", (BATCH, SEQ, P), mb.dt.float32, kind="ExternalOutput").ap())
    macaron_block(nc, *args)
    result = run_bass_kernel_spmd(nc, [arrays], core_ids=[0])
    return result.results[0]["out_0"]
```

```python
from contextlib import ExitStack

import concourse.bass as bass
from concourse import mybir


FP32 = mybir.dt.float32
FP16 = mybir.dt.float16
I32 = mybir.dt.int32
ACT = mybir.ActivationFunctionType
ALU = mybir.AluOpType
AX = mybir.AxisListType.X

P = 128
BATCH, SEQ = 4, 1024
TOK = BATCH * SEQ
GT = SEQ // P
NE, HID, TOPK = 8, 512, 2
HB = HID // P
SLOT = 256
NTILE = TOPK * TOK // SLOT + NE - 1
REG = TOK + SLOT
ROWW = P + 2
WS = 16.0
OUTSIDE = 1 << 20
BIG = 3.0e38
TWO_PI = 6.283185307179586
LOG2_E, LN2_HIGH, LN2_LOW = 1.4426950408889634, 0.693359375, -2.12194440e-4
TWO_PI_PARTS = (6.28125, 0.0019350051879882812, 3.0199159819e-7)
EPS = 1e-5
BUFS = 2
STEP = 4
PEEL = 6
H0, H1 = 1, 1 + (NTILE - PEEL) // STEP
REST = PEEL + (H1 - H0) * STEP
HALF = SEQ // 2
CHUNK = 4
NC = SEQ // CHUNK
CQ = GT // CHUNK
TURNS = SEQ.bit_length() - 1


def macaron_block(nc, x, nu_log, theta_log, b_re, b_im, c_re_t, c_im_t, d_vec, gamma_log,
                  router_t, router_b, w1_t, b1_t, w2_t, b2, out):
    ctx = ExitStack()
    with ctx:
        def sb(name, shape, dt=FP32):
            return ctx.enter_context(nc.sbuf_tensor(name, shape, dt))

        def sem(name):
            return ctx.enter_context(nc.semaphore(name))

        rows_dram = [nc.dram_tensor(f"rows{f}", [NE * REG + SLOT, ROWW], FP32, kind="Internal").ap() for f in range(2)]
        y_dram = [nc.dram_tensor(f"y{f}", [TOPK * TOK, P], FP32, kind="Internal").ap() for f in range(2)]

        xres = sb("xres", [P, BATCH, GT, P])
        yin = sb("yin", [P, 2, TOPK, GT, P])
        xn = sb("xn", [P, 2, GT, P])
        xnt = sb("xnt", [P, 3, SEQ])
        rows = sb("rows", [P, TOPK, BATCH, GT, ROWW])
        bn = sb("bn", [P, GT, 6])
        mv = sb("mv", [P, 2, GT, 2])
        newton = sb("newton", [P, 3, 2, GT])
        guess_i = sb("guess_i", [P, 2, GT], I32)
        rstd = sb("rstd", [P, 2, GT])
        shift = sb("shift", [P, 2, GT])
        ident = sb("ident", [P, P])
        ident16 = sb("ident16", [P, P], FP16)
        before = sb("before", [P, P], FP16)
        ones16 = sb("ones16", [P, P], FP16)
        w1h = sb("w1h", [P, NE * 2 * HID], FP16)
        w1l = sb("w1l", [P, NE * 2 * HID], FP16)
        w2h = sb("w2h", [P, NE * HB * P], FP16)
        w2l = sb("w2l", [P, NE * HB * P], FP16)
        wst = sb("wst", [P, 2, 2 * HID + HB * P])
        b1g = sb("b1g", [P, NE, 2 * HB])
        bias = sb("bias", [P, STEP, 2 * HB])
        b2p = sb("b2p", [2, NE * P], FP16)
        rwt = sb("rwt", [P, NE])
        rbb = sb("rbb", [P, NE])
        rev_i = sb("rev_i", [P, 2 * NE + NTILE], I32)
        rev_f = sb("rev_f", [P, 2 * NE + NTILE])
        dest_i = sb("dest_i", [P, TOPK, BATCH, GT], I32)
        lg = sb("lg", [P, GT, NE])
        m1 = sb("m1", [P, GT])
        m2 = sb("m2", [P, GT])
        rr = sb("rr", [P, GT])
        oh1 = sb("oh1", [P, GT, NE])
        oh2 = sb("oh2", [P, GT, NE])
        tmp8 = sb("tmp8", [P, GT, NE])
        oh = sb("oh", [P, 2, GT, NE], FP16)
        seen = sb("seen", [P, 2, BATCH + 1, NE], FP16)
        seen1 = sb("seen1", [P, NE])
        dif = sb("dif", [P, 2, GT])
        edif = sb("edif", [P, 2, GT])
        den = sb("den", [P, GT])
        wk = sb("wk", [P, TOPK, GT])
        slotf = sb("slotf", [P, GT, NE])
        slot1 = sb("slot1", [P, GT])
        slot_i = sb("slot_i", [P, TOPK, 2, BATCH, GT], I32)
        cnt = sb("cnt", [P, NE])
        cnt_i = sb("cnt_i", [P, NE], I32)
        ntile = sb("ntile", [P, NE])
        upto = sb("upto", [P, NE])
        ones8 = sb("ones8", [P, NE])
        unused = sb("unused", [P, 4])
        base8 = sb("base8", [P, NE])
        toff = sb("toff", [P, NTILE])
        tex = sb("tex", [P, NTILE])
        toff_i = sb("toff_i", [P, 2, NTILE], I32)
        tex_i = sb("tex_i", [P, 2, NTILE], I32)
        pad_i = sb("pad_i", [P, 2, NE], I32)
        padrow = sb("padrow", [P, 2, ROWW])
        xt = sb("xt", [P, STEP, 2, ROWW])
        dest = sb("dest", [P, STEP, 2], I32)
        weight = sb("weight", [P, STEP, 2])
        xt_t = sb("xt_t", [P, BUFS, 2, SLOT], FP16)
        gate = sb("gate", [P, HB, SLOT])
        act = sb("act", [P, HB, SLOT])
        yout = sb("yout", [P, STEP, 2, P])
        b_pow = sb("b_pow", [P, 2, CHUNK, P])
        bt_pow = sb("bt_pow", [P, 2, CHUNK, P])
        c_pow = sb("c_pow", [P, 2, CHUNK + 1, P])
        k_lag = sb("k_lag", [P, CHUNK, P])
        diag_d = sb("diag_d", [P, P])
        vec = sb("vec", [P, 4])
        lam = sb("lam", [P, 3])
        double = sb("double", [P, TURNS])
        trig = sb("trig", [P, 8, TURNS])
        turns_i = sb("turns_i", [P, TURNS], I32)
        ex = sb("ex", [P, 3, 4])
        ex_i = sb("ex_i", [P, 2, 4], I32)
        radius = sb("radius", [P, 3])
        power = sb("power", [P, 4, CHUNK])
        ctab = sb("ctab", [P, NC])
        stab = sb("stab", [P, NC])
        states = sb("states", [P, 2, 2, NC + 1])
        b2b = yin[0:2, 0, :, :, :].rearrange("p k t d -> p k (t d)")
        b2h = yin[0:2, 1, :, :, :].rearrange("p k t d -> p k (t d)").bitcast(FP16)
        ge_hi, ge_lo = [b[:, :, :].rearrange("p j s -> p (j s)")[:, 0:NTILE * NE].rearrange("p (t e) -> p t e", e=NE)
                        for b in (gate, act)]
        gate_flat, act_flat = [b[:, :, :].rearrange("p j s -> p (j s)") for b in (gate, act)]
        rot = [gate_flat[:, i * NC:(i + 1) * NC] for i in range(4)]
        yre, yim = [act_flat[:, i * NC:(i + 1) * NC] for i in range(2)]
        scaled = [b[:, i * P:(i + 1) * P] for b in (gate_flat, act_flat) for i in range(2 * HID // P)]
        acth = sb("acth", [P, BUFS, HB, SLOT], FP16)
        actl = sb("actl", [P, BUFS, HB, SLOT], FP16)

        bank = [ctx.enter_context(nc.psum_tensor(f"bank{i}", [P, 512], FP32)) for i in range(8)]
        up_ps, y_ps, t_ps = bank[0:4], bank[4:6], bank[6:8]
        rows16 = rows[:, :, :, :, 0:P].bitcast(FP16)
        xt16 = xt[:, :, :, 0:P].bitcast(FP16)
        logit_ps, rank_ps = bank[2], bank[3]
        t16 = [t[:, :].bitcast(FP16) for t in t_ps]

        s_xin = [sem(f"s_xin{g}") for g in range(BATCH)]
        s_small = sem("s_small")
        s_w = [sem(f"s_w{i}") for i in range(2)]
        s_pool = sem("s_pool")
        s_b2 = sem("s_b2")
        s_ident16 = sem("s_ident16")
        s_ones = sem("s_ones")
        s_wh = sem("s_wh")
        s_wl = sem("s_wl")
        s_b1u = sem("s_b1u")
        s_rstd = sem("s_rstd")
        s_xn = sem("s_xn")
        s_tr = sem("s_tr")
        s_xnt = sem("s_xnt")
        s_hi = sem("s_hi")
        s_low = sem("s_low")
        s_ypair = sem("s_ypair")
        s_logit = sem("s_logit")
        s_seen = sem("s_seen")
        s_dif = sem("s_dif")
        s_edif = sem("s_edif")
        s_oh = sem("s_oh")
        s_rank = sem("s_rank")
        s_slot = sem("s_slot")
        s_sent = sem("s_sent")
        s_cnt = sem("s_cnt")
        s_tab = sem("s_tab")
        s_pad = sem("s_pad")
        s_chain = sem("s_chain")
        s_xt = [sem(f"s_xt{i}") for i in range(STEP)]
        s_t = sem("s_t")
        s_xtt = sem("s_xtt")
        s_dest = sem("s_dest")
        s_bias = [sem(f"s_bias{i}") for i in range(STEP)]
        s_up = [sem(f"s_up{j}") for j in range(HB)]
        s_gate = [sem(f"s_gate{j}") for j in range(HB)]
        s_act = [sem(f"s_act{j}") for j in range(HB)]
        s_acth = [sem(f"s_acth{i}") for i in range(2)]
        s_actl = [sem(f"s_actl{i}") for i in range(2)]
        s_down = sem("s_down")
        s_yout = sem("s_yout")
        s_ygo = sem("s_ygo")
        s_xgo = sem("s_xgo")
        s_ysent = [sem(f"s_ysent{i}") for i in range(STEP)]
        s_yin = [[sem(f"s_yin{i}_{k}") for k in range(TOPK)] for i in range(2)]
        s_x1 = sem("s_x1")
        s_x1_pool = sem("s_x1_pool")
        s_row = sem("s_row")
        s_bpow = sem("s_bpow")
        s_btr = sem("s_btr")
        s_bt = sem("s_bt")
        s_bu = sem("s_bu")
        s_bud = sem("s_bud")
        s_prod = sem("s_prod")
        s_cx = sem("s_cx")
        s_x2 = sem("s_x2")
        s_out = sem("s_out")

        order = [("ffn", 0, g) for g in range(BATCH)]
        order += [("lru", 0, 0), ("lru", 0, 1)]
        for g in range(BATCH):
            order += [("ffn", 1, g)] + ([("lru", 0, g + 2)] if g + 2 < BATCH else [])
        number = {inst: n for n, inst in enumerate(order)}

        def xnt_of(n):
            kind, f, g = order[n]
            return g % 2 if kind == "lru" else 2

        def sent_before(f, tile):
            count = lambda n: (n - tile % STEP + STEP - 1) // STEP
            return f * count(NTILE) + count(tile)

        def added(n):
            if 0 < n < BATCH:
                return s_x1_pool, n
            return s_x1, 1 if n == 0 else n - BATCH + 2

        def wait(eng, semaphore, value):
            if not (isinstance(value, int) and value <= 0):
                eng.wait_ge(semaphore, value)

        def expert_tiles(eng, f, tile):
            def peeled(t):
                tile(t, t, lambda u: f * NTILE + t + u, lambda u, each: each * sent_before(f, t + u))

            for t in range(PEEL):
                peeled(t)
            with eng.Fori(H0, H1) as h:
                made = {}

                def value(step, const):
                    if (step, const) not in made:
                        made[step, const] = eng.snap(h * step + const)
                    return made[step, const]

                for t in range(PEEL, PEEL + STEP):
                    tile(t, value(STEP, t - STEP), lambda u: value(STEP, f * NTILE + t + u - STEP),
                         lambda u, each: value(each, each * (sent_before(f, t + u) - 1)))
            for t in range(REST, NTILE):
                peeled(t)

        block = ctx.enter_context(nc.Block())

        @block.sync
        def _(sp):
            small = [(rwt[:, :], router_t), (rbb[:, :], router_b.partition_broadcast(P)),
                     (b1g[:, :, :], b1_t), (b2b[:, 0, :], b2.partition_broadcast(2)),
                     (b_pow[:, 0, 0, :], b_re), (b_pow[:, 1, 0, :], b_im),
                     (c_pow[:, 0, 0, :], c_re_t), (c_pow[:, 1, 0, :], c_im_t),
                     (vec[:, 0:1], nu_log), (vec[:, 1:2], theta_log), (vec[:, 3:4], d_vec), (vec[:, 2:3], gamma_log)]
            for g in range(BATCH):
                for c in range(2):
                    ts = slice(c * GT // 2, (c + 1) * GT // 2)
                    sp.dma_start(xres[:, g, ts, :], x[g].rearrange("(p t) d -> p t d", p=P)[:, ts, :])\
                        .then_inc(s_xin[g], 16)
                if g == 0:
                    for dst, src in small:
                        sp.dma_start(dst, src).then_inc(s_small, 16)
            for e in range(NE):
                if e >= 2:
                    sp.wait_ge(s_wl, 2 * (e - 1))
                sp.dma_start(wst[:, e % 2, 0:2 * HID], w1_t[:, e, :]).then_inc(s_w[e % 2], 16)
                sp.dma_start(wst[:, e % 2, 2 * HID:], w2_t[:, e, :]).then_inc(s_w[e % 2], 16)

            for f in range(2):
                sp.wait_ge(s_tab, f + 1)
                for e in range(NE):
                    row0 = sp.value_load(pad_i[0:1, f, e:e + 1], min_val=0, max_val=NE * REG - SLOT)
                    sp.dma_start(rows_dram[f][bass.ds(row0, SLOT), :].rearrange("(p r) w -> p r w", r=2),
                                 padrow[:, :, :]).then_inc(s_pad, 16)
                sp.dma_start(rows_dram[f][NE * REG:NE * REG + SLOT, :].rearrange("(p r) w -> p r w", r=2),
                             padrow[:, :, :]).then_inc(s_pad, 16)

                def load(t, s, n, dma):
                    row0 = sp.value_load(toff_i[0:1, f, bass.ds(s, 1)], min_val=0, max_val=NE * REG)
                    if t == 0:
                        sp.wait_ge(s_pad, 16 * (NE + 1) * (f + 1))
                        sp.wait_ge(s_sent, 16 * TOPK * BATCH * GT * (f + 1))
                    wait(sp, s_t, n(1 - STEP))
                    wait(sp, s_dest, n(1 - STEP))
                    sp.dma_start(xt[:, t % STEP, :, :],
                                 rows_dram[f][bass.ds(row0, SLOT), :].rearrange("(p r) w -> p r w", r=2))\
                        .then_inc(s_xt[t % STEP], 16)
                    expert = sp.value_load(tex_i[0:1, f, bass.ds(s, 1)], min_val=0, max_val=NE - 1)
                    wait(sp, s_act[HB - 1], n(1 - STEP))
                    sp.dma_start(bias[:, t % STEP, :].unsqueeze(1), b1g[:, bass.ds(expert, 1), :])\
                        .then_inc(s_bias[t % STEP], 16)

                sp.wait_ge(s_b1u, 1)
                expert_tiles(sp, f, load)
                for t in range(NTILE - STEP, NTILE):
                    sp.wait_ge(s_ysent[t % STEP], 32 * (sent_before(f, t) + 1))
                for g in range(BATCH):
                    n = f * BATCH + g
                    if n >= 2:
                        sp.wait_ge(*added(n - 2))
                    for k in range(TOPK):
                        sp.dma_start(yin[:, n % 2, k, :, :],
                                     y_dram[f].rearrange("(k b p t) d -> k b p t d", k=TOPK, b=BATCH, p=P)[k, g])\
                            .then_inc(s_yin[n % 2][k], 16)
            for g in range(BATCH):
                sp.wait_ge(*added(BATCH + g))
                sp.dma_start(out[g].rearrange("(p t) d -> p t d", p=P), xres[:, g, :, :]).then_inc(s_out, 16)
            sp.wait_ge(s_out, 16 * BATCH)

        @block.gpsimd
        def _(pool):
            pool.memset(ident[:, :], 0.0).then_inc(s_pool, 1)
            pool.memset(before[:, :], 1.0).then_inc(s_pool, 1)
            pool.iota(rev_i[:, 0:NE], pattern=[[-1, NE]], base=NE, channel_multiplier=0).then_inc(s_pool, 1)
            pool.iota(rev_i[:, NE:2 * NE], pattern=[[REG, NE]], base=0, channel_multiplier=0).then_inc(s_pool, 1)
            pool.iota(rev_i[:, 2 * NE:], pattern=[[1, NTILE]], base=0, channel_multiplier=0).then_inc(s_pool, 1)
            pool.iota(dest_i[:, :, :, :], pattern=[[TOK, TOPK], [SEQ, BATCH], [1, GT]], base=0,
                      channel_multiplier=GT).then_inc(s_pool, 1)
            pool.wait_ge(s_pool, 2)
            pool.affine_select(out=ident[:, :], in_=ident[:, :], compare_op=ALU.not_equal, fill=1.0, base=0,
                               pattern=[[-1, P]], channel_multiplier=1).then_inc(s_pool, 1)
            pool.affine_select(out=before[:, :], in_=before[:, :], compare_op=ALU.is_gt, fill=0.0, base=0,
                               pattern=[[1, P]], channel_multiplier=-1).then_inc(s_pool, 1)
            pool.memset(ones16[:, :], 1.0).then_inc(s_pool, 1)
            for m in range(TURNS):
                ins = pool.memset(double[:, m:m + 1], float(1 << m))
            ins.then_inc(s_pool, 1)

            def send_rows(f, g):
                pool.wait_ge(s_slot, f * BATCH + g + 1)
                for k in range(TOPK):
                    if k > 0:
                        pool.wait_ge(s_row, f * BATCH + g + 1)
                    for t in range(GT):
                        pool.indirect_dma_start(
                            out=rows_dram[f],
                            out_offset=bass.IndirectOffsetOnAxis(ap=slot_i[:, k, f, g, t:t + 1], axis=0),
                            in_=rows[:, k, g, t, :], in_offset=None).then_inc(s_sent, 16)

            last_row = pool.to_reg(TOPK * TOK - 1)

            def take_meta(t, n, dma):
                pool.wait_ge(s_xt[t % STEP], dma(STEP, 16))
                wait(pool, s_ysent[t % STEP], dma(0, 32))
                pool.sem_inc(s_xgo, 1)
                pool.tensor_copy(dest[:, t % STEP, :], xt[:, t % STEP, :, P])
                pool.tensor_copy(weight[:, t % STEP, :], xt[:, t % STEP, :, P + 1]).then_inc(s_dest, 1)

            def send_y(f, t, n):
                pool.wait_ge(s_yout, n(1))
                pool.sem_inc(s_ygo, 1)
                for r in range(2):
                    pool.indirect_dma_start(
                        out=y_dram[f],
                        out_offset=bass.IndirectOffsetOnAxis(ap=dest[:, t % STEP, r:r + 1], axis=0),
                        in_=yout[:, t % STEP, r, :], in_offset=None, bounds_check=last_row,
                        oob_is_err=False).then_inc(s_ysent[t % STEP], 16)

            def pair_outputs(f, g):
                n = f * BATCH + g
                for k in range(TOPK):
                    pool.wait_ge(s_yin[n % 2][k], 16 * (n // 2 + 1))
                pool.tensor_tensor(yin[:, n % 2, 0, :, :], yin[:, n % 2, 0, :, :], yin[:, n % 2, 1, :, :],
                                   ALU.add).then_inc(s_ypair, 1)

            def add_outputs(f, g):
                n = f * BATCH + g
                pool.wait_ge(s_ypair, n + 1)
                pool.tensor_tensor(xres[:, g, :, :], xres[:, g, :, :], yin[:, n % 2, 0, :, :], ALU.add)\
                    .then_inc(s_x1_pool, 1)

            for f in range(2):
                for g in range(BATCH):
                    send_rows(f, g)
                take_meta(0, lambda u: f * NTILE + u, lambda u, each: each * sent_before(f, u))

                def tile(t, s, n, dma):
                    if t + 1 < NTILE:
                        take_meta(t + 1, lambda u: n(u + 1), lambda u, each: dma(u + 1, each))
                    send_y(f, t, n)

                expert_tiles(pool, f, tile)
                for g in range(BATCH if f == 0 else 0):
                    pair_outputs(f, g)
                    if g > 0:
                        add_outputs(f, g)

        @block.scalar
        def _(act_e):
            def normalise(n):
                kind, f, g = order[n]
                act_e.wait_ge(s_rstd, n + 1)
                if n >= 2:
                    act_e.wait_ge(s_tr, 2 * (n - 1))
                    kind2, f2, g2 = order[n - 2]
                    if kind2 == "ffn":
                        act_e.wait_ge(s_low, f2 * BATCH + g2 + 1)
                for t in range(GT):
                    ins = nc.scalar.activation(xn[:, n % 2, t, :], xres[:, g, t, :], ACT.Identity,
                                               scale=rstd[:, n % 2, t:t + 1], bias=shift[:, n % 2, t:t + 1])
                    if t % 4 == 3:
                        ins.then_inc(s_xn, 1)

            def transposed(n):
                kind, f, g = order[n]
                if kind == "ffn" and f * BATCH + g > 0:
                    act_e.wait_ge(s_logit, f * BATCH + g)
                if kind == "lru" and g >= 2:
                    act_e.wait_ge(s_cx, 2 * (g - 1))
                for c in range(2):
                    act_e.wait_ge(s_tr, 2 * n + c + 1)
                    nc.scalar.copy(xnt[:, xnt_of(n), c * HALF:(c + 1) * HALF], t_ps[c][:, :]).then_inc(s_xnt, 1)

            def high_part(f, g):
                n = number["ffn", f, g]
                act_e.wait_ge(s_xn, 2 * n + 2)
                if f > 0:
                    act_e.wait_ge(s_sent, 16 * TOPK * BATCH * GT)
                nc.scalar.copy(rows16[:, 0, g, :, 0:P], xn[:, n % 2, :, :]).then_inc(s_hi, 1)

            def rows_of(f, g):
                normalise(number["ffn", f, g])
                transposed(number["ffn", f, g])
                high_part(f, g)

            def table_for(function, n):
                nc.scalar.activation(unused[:, n:n + 1], ones8[:, 0:1], function)

            def second_row(f, g):
                act_e.wait_ge(s_low, f * BATCH + g + 1)
                nc.scalar.copy(rows16[:, 1, g, :, :], rows16[:, 0, g, :, :]).then_inc(s_row, 1)

            def exp_dif(f, g):
                q = f * BATCH + g
                act_e.wait_ge(s_dif, q + 1)
                nc.scalar.activation(edif[:, q % 2, :], dif[:, q % 2, :], ACT.Exp).then_inc(s_edif, 1)

            def weight_high(e):
                act_e.wait_ge(s_w[e % 2], 32 * (e // 2 + 1))
                nc.scalar.mul(w1h[:, e * 2 * HID:(e + 1) * 2 * HID], wst[:, e % 2, 0:2 * HID], WS).then_inc(s_wh, 1)
                nc.scalar.mul(w2h[:, e * HB * P:(e + 1) * HB * P], wst[:, e % 2, 2 * HID:], WS).then_inc(s_wh, 1)

            act_e.wait_ge(s_ones, 1)
            table_for(ACT.Exp, 0)
            rows_of(0, 0)
            for g in range(BATCH):
                if g + 1 < BATCH:
                    rows_of(0, g + 1)
                exp_dif(0, g)
                second_row(0, g)
                for e in (2 * g, 2 * g + 1):
                    weight_high(e)
            nc.scalar.mul(b2b[:, 1, :], b2b[:, 0, :], WS * WS).then_inc(s_b2, 1)
            act_e.wait_ge(s_b2, 1)
            nc.scalar.copy(b2h[:, 0, 0:NE * P], b2b[:, 1, :]).then_inc(s_b2, 1)
            act_e.wait_ge(s_b2, 2)
            nc.scalar.mul(b2h[:, 1, 0:NE * P], b2h[:, 0, 0:NE * P], ident[0:2, 0:1]).then_inc(s_b2, 1)

            def gates(t, j, n):
                act_e.wait_ge(s_up[j], n(1))
                nc.scalar.activation(gate[:, j, :], up_ps[j][:, 0:SLOT], ACT.Silu, scale=1.0 / WS,
                                     bias=bias[:, t % STEP, j:j + 1]).then_inc(s_gate[j], 1)

            def act_high(t, half, n):
                act_e.wait_ge(s_act[2 * half + 1], n(1))
                if half == 0:
                    wait(act_e, s_down, n(1 - BUFS))
                nc.scalar.copy(acth[:, t % BUFS, 2 * half:2 * half + 2, :],
                               act[:, 2 * half:2 * half + 2, :]).then_inc(s_acth[half], 1)

            def weighted(t, n, dma):
                act_e.wait_ge(s_dest, n(1))
                wait(act_e, s_ysent[t % STEP], dma(0, 32))
                act_e.wait_ge(s_down, n(1))
                for r in range(2):
                    ins = nc.scalar.mul(yout[:, t % STEP, r, :], y_ps[t % BUFS][:, r * P:(r + 1) * P],
                                        weight[:, t % STEP, r:r + 1])
                ins.then_inc(s_yout, 1)

            def tile(t, s, n, dma):
                act_e.wait_ge(s_bias[t % STEP], dma(STEP, 16))
                gates(t, 0, n)
                gates(t, 1, n)
                gates(t, 2, n)
                act_high(t, 0, n)
                gates(t, 3, n)
                act_high(t, 1, n)
                if t >= 1:
                    weighted(t - 1, lambda u: n(u - 1), lambda u, each: dma(u - 1, each))

            for f in range(2):
                if f > 0:
                    table_for(ACT.Exp, 2)
                    for i in range(2):
                        act_e.wait_ge(s_btr, i + 1)
                        nc.scalar.copy(bt_pow[:, i, :, :].rearrange("p k d -> p (k d)"),
                                       y_ps[i][:, :]).then_inc(s_bt, 1)
                    act_e.wait_ge(s_btr, 3)
                    nc.scalar.copy(k_lag[:, :, :].rearrange("p k d -> p (k d)"), up_ps[3][:, :]).then_inc(s_bt, 1)
                    for g in range(2):
                        normalise(number["lru", 0, g])
                        transposed(number["lru", 0, g])
                    for g in range(BATCH):
                        rows_of(1, g)
                        if g + 2 < BATCH:
                            normalise(number["lru", 0, g + 2])
                            transposed(number["lru", 0, g + 2])
                        exp_dif(1, g)
                        second_row(1, g)
                table_for(ACT.Silu, 1 + 2 * f)
                act_e.wait_ge(s_tab, f + 1)

                expert_tiles(act_e, f, tile)
                t = NTILE - 1
                weighted(t, lambda u: f * NTILE + t + u, lambda u, each: each * sent_before(f, t + u))

        @block.vector
        def _(dve):
            count = [0]

            def link(ins):
                count[0] += 1
                ins.then_inc(s_chain, 1)
                dve.wait_ge(s_chain, count[0])

            V = nc.vector

            def over_e(a):
                return a.unsqueeze(2).to_broadcast([P, GT, NE])

            def over_t(a):
                return a.unsqueeze(1).to_broadcast([P, GT, NE])

            V.memset(ones8[:, :], 1.0).then_inc(s_ones, 1)
            V.memset(seen[:, :, 0, :], 0.0)
            link(V.memset(padrow[:, :, :], 0.0))
            link(V.memset(padrow[:, :, P:P + 1], float(OUTSIDE)))
            dve.wait_ge(s_pool, 9)
            V.tensor_copy(ident16[:, :], ident[:, :]).then_inc(s_ident16, 1)
            link(V.tensor_copy(rev_f[:, :], rev_i[:, :]))
            for k in range(TOPK):
                for g in range(BATCH):
                    ins = V.tensor_copy(rows[:, k, g, :, P:P + 1],
                                        dest_i[:, k, g, :].unsqueeze(2))
            link(ins)

            def measure(n):
                kind, f, g = order[n]
                for t in range(GT):
                    ins = V.bn_stats(bn[:, t, :], xres[:, g, t, :])
                link(ins)
                for t in range(GT):
                    ins = V.bn_aggr(mv[:, n % 2, t, :], bn[:, t, :])
                link(ins)

            def scales(n, count):
                if n + count > 2:
                    dve.wait_ge(s_xn, 2 * (n + count - 2))
                of = slice(n % 2, n % 2 + count)
                r, r_i, half_i = rstd[:, of, :], rstd[:, of, :].bitcast(I32), guess_i[:, of, :]
                v, square, minus_half_v = [newton[:, i, of, :] for i in range(3)]
                link(V.tensor_scalar(v, mv[:, of, :, 1], EPS, None, ALU.add))
                V.tensor_scalar(minus_half_v, v, -0.5, None, ALU.mult)
                link(V.tensor_scalar(half_i, v.bitcast(I32), 1, None, ALU.logical_shift_right))
                link(V.tensor_scalar(r_i, half_i, -1.0, float(0x5f3759df), ALU.mult, ALU.add))
                for _ in range(3):
                    link(V.tensor_tensor(square, r, r, ALU.mult))
                    link(V.tensor_tensor(square, square, minus_half_v, ALU.mult))
                    link(V.scalar_tensor_tensor(r, square, 1.5, r, ALU.add, ALU.mult))
                V.scalar_tensor_tensor(shift[:, of, :], mv[:, of, :, 0], -1.0, r, ALU.mult, ALU.mult)\
                    .then_inc(s_rstd, count)

            def statistics(n):
                measure(n)
                scales(n, 1)

            def row_parts(f, g):
                n = number["ffn", f, g]
                dve.wait_ge(s_hi, f * BATCH + g + 1)
                V.tensor_tensor(rows16[:, 0, g, :, P:2 * P], xn[:, n % 2, :, :], rows16[:, 0, g, :, 0:P],
                                ALU.subtract).then_inc(s_low, 1)

            def pick(o, m):
                link(V.tensor_reduce(m[:, :], lg[:, :, :], AX, ALU.max))
                link(V.tensor_tensor(tmp8[:, :, :], lg[:, :, :], over_e(m[:, :]), ALU.is_ge))
                link(V.tensor_tensor(tmp8[:, :, :], tmp8[:, :, :], over_t(rev_f[:, 0:NE]), ALU.mult))
                link(V.tensor_reduce(rr[:, :], tmp8[:, :, :], AX, ALU.max))
                link(V.tensor_tensor(o[:, :, :], tmp8[:, :, :], over_e(rr[:, :]), ALU.is_equal))

            def choose(f, g):
                q = f * BATCH + g
                dve.wait_ge(s_logit, q + 1)
                link(V.tensor_tensor(lg[:, :, :], logit_ps[:, 0:GT * NE].rearrange("p (t e) -> p t e", e=NE),
                                     over_t(rbb[:, :]), ALU.add))
                pick(oh1, m1)
                link(V.scalar_tensor_tensor(lg[:, :, :].rearrange("p t e -> p (t e)"),
                                            oh1[:, :, :].rearrange("p t e -> p (t e)"), -BIG,
                                            lg[:, :, :].rearrange("p t e -> p (t e)"), ALU.mult, ALU.add))
                pick(oh2, m2)
                V.tensor_tensor(dif[:, q % 2, :], m2[:, :], m1[:, :], ALU.subtract).then_inc(s_dif, 1)
                V.tensor_tensor(oh[:, q % 2, :, :], oh1[:, :, :], oh2[:, :, :], ALU.add).then_inc(s_oh, 1)
                dve.wait_ge(s_oh, q + 1)
                link(V.tensor_reduce(seen1[:, :], oh[:, q % 2, :, :].rearrange("p t e -> p e t"), AX, ALU.add))
                V.tensor_tensor(seen[:, f, g + 1, :], seen[:, f, g, :], seen1[:, :], ALU.add).then_inc(s_seen, 1)

            def weights_and_slots(f, g):
                q = f * BATCH + g
                dve.wait_ge(s_edif, q + 1)
                link(V.tensor_scalar(den[:, :], edif[:, q % 2, :], 1.0, 2.0 * WS * WS, ALU.add, ALU.mult))
                link(V.reciprocal(wk[:, 0, :], den[:, :]))
                link(V.tensor_tensor(wk[:, 1, :], wk[:, 0, :], edif[:, q % 2, :], ALU.mult))
                for k in range(TOPK):
                    link(V.tensor_copy(rows[:, k, g, :, P + 1:P + 2], wk[:, k, :].unsqueeze(2)))
                dve.wait_ge(s_rank, q + 1)
                link(V.tensor_tensor(slotf[:, :, :], rank_ps[:, 0:GT * NE].rearrange("p (t e) -> p t e", e=NE),
                                     over_t(rev_f[:, NE:2 * NE]), ALU.add))
                for k, o in enumerate((oh1, oh2)):
                    link(V.tensor_tensor(tmp8[:, :, :], slotf[:, :, :], o[:, :, :], ALU.mult))
                    link(V.tensor_reduce(slot1[:, :], tmp8[:, :, :], AX, ALU.add))
                    ins = V.tensor_copy(slot_i[:, k, f, g, :], slot1[:, :])
                    if k == 0:
                        link(ins)
                ins.then_inc(s_slot, 1)

            def tile_table(f):
                dve.wait_ge(s_cnt, f + 1)
                link(V.tensor_copy(cnt[:, :], rank_ps[:, 128:128 + NE]))
                link(V.tensor_scalar(cnt_i[:, :], cnt[:, :], float(SLOT - 1), None, ALU.add))
                link(V.tensor_scalar(cnt_i[:, :], cnt_i[:, :], SLOT.bit_length() - 1, None, ALU.logical_shift_right))
                link(V.tensor_copy(ntile[:, :], cnt_i[:, :]))
                link(V.tensor_tensor_scan(upto[:, :], ones8[:, :], ntile[:, :], 0.0, ALU.mult, ALU.add))
                link(V.tensor_tensor(pad_i[:, f, :], cnt[:, :], rev_f[:, NE:2 * NE], ALU.add))
                tiles = rev_f[:, 2 * NE:]

                def grid(a):
                    return a.unsqueeze(1).to_broadcast([P, NTILE, NE])

                link(V.tensor_tensor(ge_hi[:, :, :], tiles.unsqueeze(2).to_broadcast([P, NTILE, NE]),
                                     grid(upto[:, :]), ALU.is_ge))
                link(V.tensor_reduce(tex[:, :], ge_hi[:, :, :], AX, ALU.add))
                link(V.tensor_tensor(ntile[:, :], upto[:, :], ntile[:, :], ALU.subtract))
                link(V.tensor_tensor(ge_lo[:, :, :], tiles.unsqueeze(2).to_broadcast([P, NTILE, NE]),
                                     grid(ntile[:, :]), ALU.is_ge))
                link(V.tensor_tensor(ge_lo[:, :, :], ge_lo[:, :, :], ge_hi[:, :, :], ALU.subtract))
                link(V.scalar_tensor_tensor(base8[:, :], ntile[:, :], -float(SLOT), rev_f[:, NE:2 * NE],
                                            ALU.mult, ALU.add))
                link(V.tensor_tensor(ge_lo[:, :, :], ge_lo[:, :, :], grid(base8[:, :]), ALU.mult))
                link(V.tensor_reduce(toff[:, :], ge_lo[:, :, :], AX, ALU.add))
                link(V.scalar_tensor_tensor(toff[:, :], tiles, float(SLOT), toff[:, :], ALU.mult, ALU.add))
                unused = ge_hi[:, :, NE - 1]
                link(V.scalar_tensor_tensor(ge_lo[:, :, 0], tiles, -float(SLOT), unused, ALU.mult, ALU.mult))
                link(V.scalar_tensor_tensor(ge_lo[:, :, 0], unused, float(NE * REG), ge_lo[:, :, 0],
                                            ALU.mult, ALU.add))
                link(V.tensor_tensor(toff_i[:, f, :], toff[:, :], ge_lo[:, :, 0], ALU.add))
                V.tensor_scalar(tex_i[:, f, :], tex[:, :], float(NE - 1), None, ALU.min).then_inc(s_tab, 1)
                dve.wait_ge(s_tab, f + 1)

            def weight_low(e):
                for i, (hi, lo, a, b) in enumerate(((w1h, w1l, 0, 2 * HID), (w2h, w2l, 2 * HID, 2 * HID + HB * P))):
                    w = b - a
                    dve.wait_ge(s_wh, 2 * e + i + 1)
                    V.scalar_tensor_tensor(lo[:, e * w:(e + 1) * w], wst[:, e % 2, a:b], WS, hi[:, e * w:(e + 1) * w],
                                           ALU.mult, ALU.subtract).then_inc(s_wl, 1)

            def horner(acc, z, coefficients):
                link(V.tensor_scalar(acc, z, coefficients[0], None, ALU.mult))
                for c in coefficients[1:-1]:
                    link(V.scalar_tensor_tensor(acc, acc, c, z, ALU.add, ALU.mult))
                link(V.tensor_scalar(acc, acc, coefficients[-1], None, ALU.add))

            def exponential(dst, src, w):
                t, k, acc = [ex[:, i, 0:w] for i in range(3)]
                k_i, two_k = [ex_i[:, i, 0:w] for i in range(2)]
                link(V.tensor_scalar(t, src, -87.0, 88.0, ALU.max, ALU.min))
                link(V.tensor_scalar(k_i, t, LOG2_E, None, ALU.mult))
                link(V.tensor_copy(k, k_i))
                link(V.scalar_tensor_tensor(t, k, -LN2_HIGH, t, ALU.mult, ALU.add))
                link(V.scalar_tensor_tensor(t, k, -LN2_LOW, t, ALU.mult, ALU.add))
                link(V.tensor_scalar(two_k, k, 127.0, float(1 << 23), ALU.add, ALU.mult))
                factorial, coefficients = 1.0, [1.0]
                for i in range(1, 10):
                    factorial *= i
                    coefficients.insert(0, 1.0 / factorial)
                horner(acc, t, coefficients)
                link(V.tensor_tensor(dst, acc, two_k.bitcast(FP32), ALU.mult))

            angle, turns, half, square, sine, cosine, c_all, s_all = [trig[:, i, :] for i in range(8)]

            def magnitudes():
                exponential(lam[:, 0:3], vec[:, 0:3], 3)
                link(V.tensor_scalar(lam[:, 0:1], lam[:, 0:1], -1.0, None, ALU.mult))
                exponential(radius[:, 0:1], lam[:, 0:1], 1)
                link(V.tensor_tensor(radius[:, 1:2], radius[:, 0:1], radius[:, 0:1], ALU.mult))
                link(V.tensor_tensor(radius[:, 2:3], radius[:, 1:2], radius[:, 1:2], ALU.mult))
                V.tensor_scalar(diag_d[:, :], ident[:, :], vec[:, 3:4], None, ALU.mult)
                for i in range(2):
                    V.tensor_scalar(b_pow[:, i, 0, :], b_pow[:, i, 0, :], lam[:, 2:3], None, ALU.mult)
                V.memset(states[:, :, :, 0:1], 0.0)
                link(V.tensor_scalar(c_pow[:, 1, 0, :], c_pow[:, 1, 0, :], -1.0, None, ALU.mult))

            def turns_of_angle():
                dve.wait_ge(s_pool, 10)
                link(V.tensor_scalar(angle, double[:, :], lam[:, 1:2], None, ALU.mult))
                link(V.tensor_scalar(turns_i[:, :], angle, 1.0 / TWO_PI, None, ALU.mult))
                link(V.tensor_copy(turns, turns_i[:, :]))
                for part in TWO_PI_PARTS:
                    link(V.scalar_tensor_tensor(angle, turns, -part, angle, ALU.mult, ALU.add))
                link(V.tensor_scalar(half, angle, 0.5, None, ALU.mult))
                link(V.tensor_tensor(square, half, half, ALU.mult))
                by_power, factorial = ([1.0], [1.0]), 1.0
                for i in range(2, 18):
                    factorial *= i
                    by_power[(i + 1) % 2].insert(0, (-1.0 if (i // 2) % 2 else 1.0) / factorial)
                of_sine, of_cosine = by_power
                pair = ((sine, of_sine), (cosine, of_cosine))
                for acc, c in pair:
                    ins = V.tensor_scalar(acc, square, c[0], None, ALU.mult)
                link(ins)
                for i in range(1, len(of_sine) - 1):
                    for acc, c in pair:
                        ins = V.scalar_tensor_tensor(acc, acc, c[i], square, ALU.add, ALU.mult)
                    link(ins)
                for acc, c in pair:
                    ins = V.tensor_scalar(acc, acc, c[-1], None, ALU.add)
                link(ins)
                link(V.tensor_tensor(sine, sine, half, ALU.mult))
                V.scalar_tensor_tensor(s_all, sine, 2.0, cosine, ALU.mult, ALU.mult)
                link(V.scalar_tensor_tensor(c_all, sine, -2.0, sine, ALU.mult, ALU.mult))
                link(V.tensor_scalar(c_all, c_all, 1.0, None, ALU.add))
                link(V.tensor_tensor(turns, c_all, c_all, ALU.mult))
                link(V.tensor_tensor(square, s_all, s_all, ALU.mult))
                link(V.tensor_tensor(square, square, turns, ALU.add))
                link(V.tensor_scalar(square, square, -0.5, 1.5, ALU.mult, ALU.add))
                V.tensor_tensor(c_all, c_all, square, ALU.mult)
                link(V.tensor_tensor(s_all, s_all, square, ALU.mult))

            def power_matrices():
                p_re, p_im, p_a, p_b = [power[:, i, :] for i in range(4)]
                V.tensor_tensor(p_re[:, 0:3], radius[:, :], c_all[:, 0:3], ALU.mult)
                link(V.tensor_tensor(p_im[:, 0:3], radius[:, :], s_all[:, 0:3], ALU.mult))
                V.tensor_tensor(p_a[:, 0:1], p_im[:, 0:1], p_im[:, 1:2], ALU.mult)
                link(V.tensor_tensor(p_b[:, 0:1], p_re[:, 0:1], p_im[:, 1:2], ALU.mult))
                V.scalar_tensor_tensor(p_re[:, 3:4], p_re[:, 0:1], p_re[:, 1:2], p_a[:, 0:1], ALU.mult, ALU.subtract)
                link(V.scalar_tensor_tensor(p_im[:, 3:4], p_im[:, 0:1], p_re[:, 1:2], p_b[:, 0:1], ALU.mult, ALU.add))
                column = {1: 0, 2: 1, 3: 3, 4: 2}
                made = [(b_pow, k, ALU.subtract, ALU.add) for k in range(1, CHUNK)]
                made += [(c_pow, k, ALU.add, ALU.subtract) for k in range(1, CHUNK + 1)]
                for n, (m, k, _, _) in enumerate(made):
                    im = p_im[:, column[k]:column[k] + 1]
                    V.tensor_scalar(scaled[2 * n], m[:, 1, 0, :], im, None, ALU.mult)
                    ins = V.tensor_scalar(scaled[2 * n + 1], m[:, 0, 0, :], im, None, ALU.mult)
                link(ins)
                for n, (m, k, op_re, op_im) in enumerate(made):
                    re = p_re[:, column[k]:column[k] + 1]
                    V.scalar_tensor_tensor(m[:, 0, k, :], m[:, 0, 0, :], re, scaled[2 * n], ALU.mult, op_re)
                    ins = V.scalar_tensor_tensor(m[:, 1, k, :], m[:, 1, 0, :], re, scaled[2 * n + 1], ALU.mult, op_im)
                link(ins)
                ins = V.tensor_copy(p_a[:, 0:1], p_re[:, 0:1])
                ins.then_inc(s_bpow, 1)

            def turn_tables():
                V.memset(ctab[:, 0:1], 1.0)
                link(V.memset(stab[:, 0:1], 0.0))
                for m in range(NC.bit_length() - 1):
                    n, a = 1 << m, m + CHUNK.bit_length() - 1
                    c_n, s_n = c_all[:, a:a + 1], s_all[:, a:a + 1]
                    V.tensor_scalar(rot[0][:, 0:n], stab[:, 0:n], s_n, None, ALU.mult)
                    link(V.tensor_scalar(rot[1][:, 0:n], ctab[:, 0:n], s_n, None, ALU.mult))
                    V.scalar_tensor_tensor(ctab[:, n:2 * n], ctab[:, 0:n], c_n, rot[0][:, 0:n],
                                           ALU.mult, ALU.subtract)
                    link(V.scalar_tensor_tensor(stab[:, n:2 * n], stab[:, 0:n], c_n, rot[1][:, 0:n],
                                                ALU.mult, ALU.add))

            def add_outputs(f, g):
                n = f * BATCH + g
                if f == 0 and g > 0:
                    dve.wait_ge(*added(n))
                    return
                dve.wait_ge(s_ypair, n + 1)
                V.tensor_tensor(xres[:, g, :, :], xres[:, g, :, :], yin[:, n % 2, 0, :, :], ALU.add).then_inc(s_x1, 1)
                dve.wait_ge(*added(n))

            def recurrence(g):
                dve.wait_ge(s_bu, g + 1)
                w_re, w_im = [ps[:, 0:NC].rearrange("n (q p) -> n p q", q=CQ) for ps in up_ps[0:2]]
                by_chunk = lambda a: a.rearrange("n (p q) -> n p q", q=CQ)
                V.tensor_tensor(by_chunk(rot[0]), by_chunk(ctab[:, :]), w_re, ALU.mult)
                V.tensor_tensor(by_chunk(rot[1]), by_chunk(stab[:, :]), w_im, ALU.mult)
                V.tensor_tensor(by_chunk(rot[2]), by_chunk(ctab[:, :]), w_im, ALU.mult)
                V.tensor_tensor(by_chunk(rot[3]), by_chunk(stab[:, :]), w_re, ALU.mult).then_inc(s_bud, 1)
                dve.wait_ge(s_bud, g + 1)
                V.tensor_tensor(rot[0], rot[0], rot[1], ALU.add)
                link(V.tensor_tensor(rot[2], rot[2], rot[3], ALU.subtract))
                decay = radius[:, 2:3].to_broadcast([P, NC])
                V.tensor_tensor_scan(yre, decay, rot[0], 0.0, ALU.mult, ALU.add)
                link(V.tensor_tensor_scan(yim, decay, rot[2], 0.0, ALU.mult, ALU.add))
                for r, y, tab in zip(rot, (yre, yim, yre, yim), (ctab, stab, stab, ctab)):
                    ins = V.tensor_tensor(r, y, tab[:, :], ALU.mult)
                link(ins)
                if g >= 2:
                    dve.wait_ge(s_cx, 2 * (g - 1))
                V.tensor_tensor(states[:, g % 2, 0, 1:], rot[0], rot[1], ALU.subtract)
                V.tensor_tensor(states[:, g % 2, 1, 1:], rot[2], rot[3], ALU.add).then_inc(s_prod, 1)
                dve.wait_ge(s_prod, g + 1)

            def add_recurrence(g):
                for c in range(2):
                    dve.wait_ge(s_cx, 2 * g + c + 1)
                    sl = xres[:, g, 4 * c:4 * c + 4, :].rearrange("p t d -> p (t d)")
                    ins = V.tensor_tensor(sl, sl, y_ps[c][:, :], ALU.add)
                ins.then_inc(s_x2, 1)
                dve.wait_ge(s_x2, g + 1)

            def first_statistics(g):
                dve.wait_ge(s_xin[g], 32)
                statistics(g)

            first_statistics(0)
            dve.wait_ge(s_small, 16 * 12)
            V.tensor_scalar(b1g[:, :, HB:2 * HB], b1g[:, :, HB:2 * HB], WS, None, ALU.mult).then_inc(s_b1u, 1)
            for g in range(BATCH):
                if g + 1 < BATCH:
                    first_statistics(g + 1)
                row_parts(0, g)
                choose(0, g)
                if g > 0:
                    weight_low(2 * g - 2)
                weights_and_slots(0, g)
                if g > 0:
                    weight_low(2 * g - 1)
            tile_table(0)
            for e in (NE - 2, NE - 1):
                weight_low(e)
            dve.wait_ge(s_b2, 3)
            link(V.tensor_tensor(b2b[:, 0, :], b2b[:, 1, :], b2h[:, 0, 0:NE * P], ALU.subtract))
            V.scalar_tensor_tensor(b2p[:, :], b2b[:, 0, :], ident[0:2, 1:2], b2h[:, 1, 0:NE * P],
                                   ALU.mult, ALU.add).then_inc(s_b2, 1)
            magnitudes()
            turns_of_angle()

            def take_tile(t, n):
                dve.wait_ge(s_t, n(1))
                V.tensor_copy(xt_t[:, t % BUFS, :, :].rearrange("p a s -> p (a s)"),
                              t16[t % BUFS][:, 0:2 * SLOT]).then_inc(s_xtt, 1)

            def activate(t, j, n):
                wait(dve, s_actl[j // 2], n(0))
                dve.wait_ge(s_gate[j], n(1))
                V.scalar_tensor_tensor(act[:, j, :], up_ps[j][:, SLOT:], bias[:, t % STEP, HB + j:HB + j + 1],
                                       gate[:, j, :], ALU.add, ALU.mult).then_inc(s_act[j], 1)

            def act_low(t, half, n):
                dve.wait_ge(s_acth[half], n(1))
                h2 = slice(2 * half, 2 * half + 2)
                V.tensor_tensor(actl[:, t % BUFS, h2, :], act[:, h2, :], acth[:, t % BUFS, h2, :],
                                ALU.subtract).then_inc(s_actl[half], 1)

            def tile(t, s, n, dma):
                if 0 < t < NTILE - 1:
                    take_tile(t + 1, lambda u: n(u + 1))
                for j in range(3):
                    activate(t, j, n)
                act_low(t, 0, n)
                activate(t, 3, n)
                if t == 0:
                    take_tile(t + 1, lambda u: n(u + 1))
                act_low(t, 1, n)

            for f in range(2):
                if f > 0:
                    power_matrices()
                    turn_tables()
                    for g in range(2):
                        add_outputs(0, g)
                        statistics(number["lru", 0, g])
                    add_outputs(0, 2)
                    measure(number["lru", 0, 2])
                    recurrence(0)
                    for g in range(BATCH):
                        ffn = number["ffn", 1, g]
                        add_recurrence(g)
                        measure(ffn)
                        scales(ffn, 2 if g + 2 < BATCH else 1)
                        if 0 < g < BATCH - 1:
                            weights_and_slots(1, g - 1)
                        if g + 1 < BATCH:
                            recurrence(g + 1)
                        if g == 0:
                            add_outputs(0, 3)
                            measure(number["lru", 0, 3])
                        row_parts(1, g)
                        choose(1, g)
                        if g >= BATCH - 2:
                            weights_and_slots(1, g)
                    tile_table(1)

                take_tile(0, lambda u: f * NTILE + u)
                expert_tiles(dve, f, tile)
            for g in range(BATCH):
                n = BATCH + g
                for k in range(TOPK):
                    dve.wait_ge(s_yin[n % 2][k], 16 * (n // 2 + 1))
                    ins = V.tensor_tensor(xres[:, g, :, :], xres[:, g, :, :], yin[:, n % 2, k, :, :], ALU.add)
                    if k < TOPK - 1:
                        link(ins)
                ins.then_inc(s_x1, 1)

        @block.tensor
        def _(pe):
            T = nc.tensor

            def transpose_rows(n):
                for c in range(2):
                    pe.wait_ge(s_xn, 2 * n + c + 1)
                    if n >= 1:
                        pe.wait_ge(s_xnt, 2 * (n - 1) + c + 1)
                    for j in range(4):
                        ins = T.transpose(t_ps[c][:, j * P:(j + 1) * P], xn[:, n % 2, 4 * c + j, :], ident[:, :])
                    ins.then_inc(s_tr, 1)

            def logits(f, g):
                n, q = number["ffn", f, g], f * BATCH + g
                pe.wait_ge(s_xnt, 2 * n + 2)
                if q >= 1:
                    pe.wait_ge(s_oh, q)
                for t in range(GT):
                    ins = T.matmul(logit_ps[:, t * NE:(t + 1) * NE], xnt[:, 2, t * P:(t + 1) * P], rwt[:, :],
                                   start=True, stop=True)
                ins.then_inc(s_logit, 1)

            def rank(f, g):
                q = f * BATCH + g
                pe.wait_ge(s_oh, q + 1)
                if q >= 1:
                    pe.wait_ge(s_slot, q)
                ranks = rank_ps[:, 0:GT * NE].rearrange("p (t e) -> p t e", e=NE)
                T.matmul(ranks, before[:, :], oh[:, q % 2, :, :], start=True, stop=False)
                for t in range(GT - 1):
                    m = GT - 1 - t
                    T.matmul(ranks[:, t + 1:, :], ones16[:, :],
                             oh[:, q % 2, t, :].unsqueeze(1).to_broadcast([P, m, NE]), start=False, stop=False)
                T.matmul(ranks, ones16[:, :], seen[:, f, g, :].unsqueeze(1).to_broadcast([P, GT, NE]),
                         start=False, stop=True).then_inc(s_rank, 1)
                if g == BATCH - 1:
                    pe.wait_ge(s_seen, q + 1)
                    pe.wait_ge(s_slot, q + 1)
                    T.matmul(rank_ps[:, 128:128 + NE], ones16[:, :], seen[:, f, BATCH, :],
                             start=True, stop=True).then_inc(s_cnt, 1)

            pe.wait_ge(s_ident16, 1)
            transpose_rows(0)
            pe.wait_ge(s_small, 16 * 12)
            for g in range(BATCH):
                logits(0, g)
                if g + 1 < BATCH:
                    transpose_rows(g + 1)
                rank(0, g)

            def lru_matrices():
                pe.wait_ge(s_bpow, 1)
                pe.wait_ge(s_yout, NTILE)
                for i in range(2):
                    for k in range(CHUNK):
                        ins = T.transpose(y_ps[i][:, k * P:(k + 1) * P], b_pow[:, i, k, :], ident[:, :])
                    ins.then_inc(s_btr, 1)
                for k in range(CHUNK):
                    o = up_ps[3][:, k * P:(k + 1) * P]
                    if k == 0:
                        T.matmul(o, ident[:, :], diag_d[:, :], start=True, stop=False)
                    T.matmul(o, b_pow[:, 0, 0, :], c_pow[:, 0, k, :], start=(k > 0), stop=False)
                    ins = T.matmul(o, b_pow[:, 1, 0, :], c_pow[:, 1, k, :], start=False, stop=True)
                ins.then_inc(s_btr, 1)

            def bu(g):
                n = number["lru", 0, g]
                pe.wait_ge(s_xnt, 2 * n + 2)
                if g > 0:
                    pe.wait_ge(s_bud, g)
                tokens = xnt[:, xnt_of(n), :].rearrange("d (q j p) -> d j q p", q=CQ, j=CHUNK)
                for i in range(2):
                    for j in range(CHUNK):
                        ins = T.matmul(up_ps[i][:, 0:NC], bt_pow[:, i, CHUNK - 1 - j, :], tokens[:, j, :, :],
                                       start=(j == 0), stop=(j == CHUNK - 1))
                ins.then_inc(s_bu, 1)

            def cx(g, from_tokens):
                if from_tokens and g > 0:
                    pe.wait_ge(s_x2, g)
                if not from_tokens:
                    pe.wait_ge(s_prod, g + 1)
                for q in range(CQ):
                    for j in range(CHUNK):
                        o = y_ps[q][:, j * P:(j + 1) * P]
                        if from_tokens:
                            for i in range(j + 1):
                                t = q * CHUNK + i
                                T.matmul(o, xnt[:, g % 2, t * P:(t + 1) * P], k_lag[:, j - i, :],
                                         start=(j == 0 and i == 0), stop=False)
                        else:
                            for i in range(2):
                                ins = T.matmul(o, states[:, g % 2, i, q:q + CQ * (P - 1) + 1:CQ],
                                               c_pow[:, i, j + 1, :], start=False,
                                               stop=(j == CHUNK - 1 and i == 1))
                    if not from_tokens:
                        ins.then_inc(s_cx, 1)

            def transpose_tile(t, n, landed):
                pe.wait_ge(s_xt[t % STEP], landed)
                for a in range(2):
                    for r in range(2):
                        ins = T.transpose(t16[t % BUFS][:, (2 * a + r) * P:(2 * a + r + 1) * P],
                                          xt16[:, t % STEP, r, a * P:(a + 1) * P], ident16[:, :])
                ins.then_inc(s_t, 1)

            def expert_of(f, s):
                return nc.values_load(tex_i[0:1, f, bass.ds(s, 1)], engines=[mybir.EngineType.PE], min_val=0,
                                      max_val=NE - 1,
                                      skip_runtime_bounds_check_because="VectorE made the table's experts: "
                                      "0 .. NE, and at most NE - 1")

            def up(e_reg, t, n):
                for j in range(HB):
                    for half in range(2):
                        at = pe.snap(e_reg * (2 * HID) + (half * HID + j * P))
                        if t < 2 and j == 0 and half == 0:
                            pe.wait_ge(s_xtt, n(1))
                        if half == 0:
                            wait(pe, s_act[j], n(0))
                        o = up_ps[j][:, half * SLOT:(half + 1) * SLOT]
                        T.matmul(o, w1h[:, bass.ds(at, P)], xt_t[:, t % BUFS, 0, :], start=True, stop=False)
                        T.matmul(o, w1h[:, bass.ds(at, P)], xt_t[:, t % BUFS, 1, :], start=False, stop=False)
                        ins = T.matmul(o, w1l[:, bass.ds(at, P)], xt_t[:, t % BUFS, 0, :], start=False, stop=True)
                    ins.then_inc(s_up[j], 1)

            def down(e_reg, t, n):
                at = [pe.snap(e_reg * (HB * P) + c * P) for c in range(HB)]
                bias_at = pe.snap(e_reg * P)
                pe.wait_ge(s_actl[1], n(1))
                for r in range(2):
                    o = y_ps[t % BUFS][:, r * P:(r + 1) * P]
                    rs = slice(r * P, (r + 1) * P)
                    T.matmul(o, ones16[0:2, :], b2p[:, bass.ds(bias_at, P)], start=True, stop=False)
                    for c in range(HB):
                        T.matmul(o, acth[:, t % BUFS, c, rs], w2h[:, bass.ds(at[c], P)], start=False, stop=False)
                        T.matmul(o, acth[:, t % BUFS, c, rs], w2l[:, bass.ds(at[c], P)], start=False, stop=False)
                        ins = T.matmul(o, actl[:, t % BUFS, c, rs], w2h[:, bass.ds(at[c], P)], start=False,
                                       stop=(c == HB - 1))
                ins.then_inc(s_down, 1)

            def tile(f, t, s, n, dma, kept):
                if 0 < t < NTILE - 1:
                    transpose_tile(t + 1, lambda u: n(u + 1), dma(1 + STEP, 16))
                e_reg = expert_of(f, s)
                up(e_reg, t, n)
                if t == 0:
                    transpose_tile(t + 1, lambda u: n(u + 1), dma(1 + STEP, 16))
                if t >= 1:
                    last = kept["expert"] if t - 1 in kept else expert_of(f, s - 1)
                    down(last, t - 1, lambda u: n(u - 1))
                kept.clear()
                kept[t] = True
                kept["expert"] = e_reg

            for f in range(2):
                b = f * NTILE
                if f > 0:
                    lru_matrices()
                    transpose_rows(number["lru", 0, 0])
                    pe.wait_ge(s_bt, 2)
                    bu(0)
                    transpose_rows(number["lru", 0, 1])
                    pe.wait_ge(s_bt, 3)
                    cx(0, True)
                    cx(0, False)
                    for g in range(BATCH):
                        if g + 1 < BATCH:
                            bu(g + 1)
                            cx(g + 1, True)
                        transpose_rows(number["ffn", 1, g])
                        logits(1, g)
                        if g + 2 < BATCH:
                            transpose_rows(number["lru", 0, g + 2])
                        if g + 1 < BATCH:
                            cx(g + 1, False)
                        rank(1, g)
                else:
                    pe.wait_ge(s_wl, 2 * NE)
                    pe.wait_ge(s_b2, 4)
                pe.wait_ge(s_tab, f + 1)

                transpose_tile(0, lambda u: b + u, 16 * (sent_before(f, 0) + 1))
                kept = {}

                def run(t, s, n, dma):
                    if t in (PEEL, REST):
                        kept.clear()
                    tile(f, t, s, n, dma, kept)

                expert_tiles(pe, f, run)
                down(expert_of(f, NTILE - 1), NTILE - 1, lambda u: b + NTILE - 1 + u)


def _laid_out(inputs):
    import numpy as np
    a = {k.replace("L0_", ""): np.asarray(v) for k, v in inputs.items()}
    col = lambda v: v.reshape(P, 1)
    row = lambda v: v.reshape(-1)
    return [
        ("x", a["attn_inputs"]), ("nu_log", col(a["attn_nu_log"])), ("theta_log", col(a["attn_theta_log"])),
        ("b_re", a["attn_B_re"]), ("b_im", a["attn_B_im"]),
        ("c_re_t", a["attn_C_re"].T), ("c_im_t", a["attn_C_im"].T),
        ("d_vec", col(a["attn_D"])), ("gamma_log", col(a["attn_gamma_log"])),
        ("router_t", a["ffn_router_w"].T), ("router_b", row(a["ffn_router_b"])),
        ("w1_t", a["ffn_w1"].transpose(2, 0, 1)),
        ("b1_t", a["ffn_b1"].reshape(NE, 2 * HB, P).transpose(2, 0, 1)),
        ("w2_t", a["ffn_w2"].reshape(NE, P, HB, P).transpose(3, 0, 2, 1).reshape(P, NE, HB * P)),
        ("b2", row(a["ffn_b2"])),
    ]


def kernel(**inputs):
    import numpy as np
    import concourse.bacc as bacc
    from concourse import mybir as mb
    from concourse.bass_utils import run_bass_kernel_spmd

    nc = bacc.Bacc("TRN2", target_bir_lowering=False, num_devices=1)
    arrays, args = {}, []
    for name, a in _laid_out(inputs):
        a = np.ascontiguousarray(a)
        arrays[f"in_{name}"] = a
        args.append(nc.dram_tensor(f"in_{name}", a.shape, mb.dt.from_np(a.dtype), kind="ExternalInput").ap())
    args.append(nc.dram_tensor("out_0", (BATCH, SEQ, P), mb.dt.float32, kind="ExternalOutput").ap())
    macaron_block(nc, *args)
    result = run_bass_kernel_spmd(nc, [arrays], core_ids=[0])
    return result.results[0]["out_0"]
```
